# Optimizing a Trainium2 kernel written in Bass

```python
import numpy as np
import jax
import jax.numpy as jnp

def _softmax(x, axis=-1):
    return jax.nn.softmax(x, axis=axis)

def _gelu(x):
    return jax.nn.gelu(x, approximate=True)

def _silu(x):
    return jax.nn.silu(x)

def _sigmoid(x):
    return jax.nn.sigmoid(x)

def _layernorm(x, axis=-1, eps=1e-05):
    m = jnp.mean(x, axis=axis, keepdims=True)
    v = jnp.var(x, axis=axis, keepdims=True)
    return (x - m) / jnp.sqrt(v + eps)

def _scatter_add(tgt, idx, src, axis=0):
    return tgt.at[idx].add(src)

def _segment_sum(src, seg, n):
    return jax.ops.segment_sum(src, seg, n)
kernel_name = 'mk_conv_preact_d2_conv_nchw256_r4_49d22c'

def setup_inputs(seed: int=0):
    np.random.seed(seed)
    _w = jnp.asarray

    def _rec_inputs():
        import jax
        import jax.numpy as jnp
        _gk = jax.random.key(seed)
        x = 7.22e-05 + 1 * jax.random.normal(jax.random.fold_in(_gk, 1), (8, 64, 16, 16), jnp.float32)
        return x
    x = _rec_inputs()

    def _L0_conv_setup():
        import jax, jax.numpy as jnp
        import numpy as np
        B, C, H, W = (8, 64, 16, 16)
        OUT_C = 64
        K = 3
        DG = 1
        CPG = C // DG
        KK = K * K

        def _sample_group(img, py, px):
            Hh, Ww = (img.shape[1], img.shape[2])
            flat = img.reshape(img.shape[0], Hh * Ww)
            y0 = jnp.floor(py)
            x0 = jnp.floor(px)
            wy = py - y0
            wx = px - x0

            def gather(yi, xi):
                valid = ((yi >= 0) & (yi < Hh) & (xi >= 0) & (xi < Ww)).astype(img.dtype)
                idx = (jnp.clip(yi, 0, Hh - 1) * Ww + jnp.clip(xi, 0, Ww - 1)).astype(jnp.int32)
                v = jnp.take(flat, idx.reshape(-1), axis=1).reshape(img.shape[0], *yi.shape)
                return v * valid
            out = gather(y0, x0) * ((1.0 - wy) * (1.0 - wx)) + gather(y0, x0 + 1.0) * ((1.0 - wy) * wx) + gather(y0 + 1.0, x0) * (wy * (1.0 - wx)) + gather(y0 + 1.0, x0 + 1.0) * (wy * wx)
            return jnp.transpose(out, (1, 0, 2, 3))

        def _forward(x, w_off, b_off, w_conv):
            b = x.shape[0]
            pad = K // 2
            out = jax.lax.conv_general_dilated(x, w_off, window_strides=(1, 1), padding=[(pad, pad), (pad, pad)], dimension_numbers=('NCHW', 'OIHW', 'NCHW')) + b_off[None, :, None, None]
            o1, o2, m = jnp.split(out, 3, axis=1)
            dy = o1.reshape(b, DG, KK, H, W)
            dx = o2.reshape(b, DG, KK, H, W)
            mask = jax.nn.sigmoid(m).reshape(b, DG, KK, 1, H, W)
            ys = jnp.arange(H, dtype=x.dtype)[None, None, None, :, None]
            xs = jnp.arange(W, dtype=x.dtype)[None, None, None, None, :]
            py = ys + dy
            px = xs + dx
            xg = x.reshape(b, DG, CPG, H, W)
            sampled = jax.vmap(jax.vmap(_sample_group))(xg, py, px)
            y = sampled * mask
            y = y.reshape(b, C * KK, H, W)
            return jnp.einsum('bkhw,ok->bohw', y, w_conv)
        key = jax.random.key(seed)
        k1, k2, k3 = jax.random.split(key, 3)
        x = jax.random.normal(k1, (B, C, H, W), jnp.float32)
        w_off = jax.random.normal(k2, (DG * 3 * KK, C, K, K), jnp.float32) * 0.01
        b_off = jnp.zeros((DG * 3 * KK,), jnp.float32)
        w_conv = jax.random.normal(k3, (OUT_C, C * KK), jnp.float32) / np.sqrt(C * KK).astype(np.float32)
        return {'x': x, 'w_off': w_off, 'b_off': b_off, 'w_conv': w_conv}
    _L0_conv_all = _L0_conv_setup()
    _L0_conv_in = {k: v for k, v in _L0_conv_all.items() if k in ('w_off', 'b_off', 'w_conv')}
    del _L0_conv_all

    def _L1_conv_setup():
        import jax, jax.numpy as jnp
        import numpy as np
        GAMMA = 2.0
        EPS = 1e-08
        key = jax.random.key(seed)
        k1, k2, k3 = jax.random.split(key, 3)
        B, C, H, W_ = (4, 64, 16, 16)
        x = jax.random.normal(k1, (B, C, H, W_), dtype=jnp.float32)
        W = jax.random.normal(k2, (C, C), dtype=jnp.float32) * (1.0 / np.sqrt(C))
        b = jax.random.normal(k3, (C,), dtype=jnp.float32) * 0.01
        return {'x': x, 'W': W, 'b': b}
    _L1_conv_all = _L1_conv_setup()
    _L1_conv_in = {k: v for k, v in _L1_conv_all.items() if k in ('W', 'b')}
    del _L1_conv_all
    return {'x': x, 'L0_conv_w_off': _L0_conv_in['w_off'], 'L0_conv_b_off': _L0_conv_in['b_off'], 'L0_conv_w_conv': _L0_conv_in['w_conv'], 'L1_conv_W': _L1_conv_in['W'], 'L1_conv_b': _L1_conv_in['b']}

def reference(x, L0_conv_w_off, L0_conv_b_off, L0_conv_w_conv, L1_conv_W, L1_conv_b):
    import jax
    import jax.numpy as jnp

    def _L0_conv_ref(x, w_off, b_off, w_conv):
        import jax, jax.numpy as jnp
        import numpy as np
        B, C, H, W = (8, 64, 16, 16)
        OUT_C = 64
        K = 3
        DG = 1
        CPG = C // DG
        KK = K * K

        def _sample_group(img, py, px):
            Hh, Ww = (img.shape[1], img.shape[2])
            flat = img.reshape(img.shape[0], Hh * Ww)
            y0 = jnp.floor(py)
            x0 = jnp.floor(px)
            wy = py - y0
            wx = px - x0

            def gather(yi, xi):
                valid = ((yi >= 0) & (yi < Hh) & (xi >= 0) & (xi < Ww)).astype(img.dtype)
                idx = (jnp.clip(yi, 0, Hh - 1) * Ww + jnp.clip(xi, 0, Ww - 1)).astype(jnp.int32)
                v = jnp.take(flat, idx.reshape(-1), axis=1).reshape(img.shape[0], *yi.shape)
                return v * valid
            out = gather(y0, x0) * ((1.0 - wy) * (1.0 - wx)) + gather(y0, x0 + 1.0) * ((1.0 - wy) * wx) + gather(y0 + 1.0, x0) * (wy * (1.0 - wx)) + gather(y0 + 1.0, x0 + 1.0) * (wy * wx)
            return jnp.transpose(out, (1, 0, 2, 3))

        def _forward(x, w_off, b_off, w_conv):
            b = x.shape[0]
            pad = K // 2
            out = jax.lax.conv_general_dilated(x, w_off, window_strides=(1, 1), padding=[(pad, pad), (pad, pad)], dimension_numbers=('NCHW', 'OIHW', 'NCHW')) + b_off[None, :, None, None]
            o1, o2, m = jnp.split(out, 3, axis=1)
            dy = o1.reshape(b, DG, KK, H, W)
            dx = o2.reshape(b, DG, KK, H, W)
            mask = jax.nn.sigmoid(m).reshape(b, DG, KK, 1, H, W)
            ys = jnp.arange(H, dtype=x.dtype)[None, None, None, :, None]
            xs = jnp.arange(W, dtype=x.dtype)[None, None, None, None, :]
            py = ys + dy
            px = xs + dx
            xg = x.reshape(b, DG, CPG, H, W)
            sampled = jax.vmap(jax.vmap(_sample_group))(xg, py, px)
            y = sampled * mask
            y = y.reshape(b, C * KK, H, W)
            return jnp.einsum('bkhw,ok->bohw', y, w_conv)
        return _forward(x, w_off, b_off, w_conv)

    def _L1_conv_ref(x, W, b):
        import jax, jax.numpy as jnp
        import numpy as np
        GAMMA = 2.0
        EPS = 1e-08
        B, C, H, W_ = x.shape
        N = H * W_
        xf = x.reshape(B, C, N)
        norm = jnp.maximum(jnp.sqrt(jnp.sum(xf * xf, axis=1)), EPS)
        xn = xf / norm[:, None, :]
        sim = jnp.einsum('bcn,bcm->bnm', xn, xn)
        sim = jax.nn.relu(sim) ** GAMMA
        t = jnp.einsum('oc,bchw->bohw', W, x) + b[None, :, None, None]
        tf = t.reshape(B, C, N)
        out = jnp.einsum('bnm,bcm->bcn', sim, tf)
        return out.reshape(B, C, H, W_)

    def _gn(v, G=32, eps=1e-05):
        B_, C_, H_, W_ = v.shape
        g = v.reshape(B_, G, C_ // G, H_, W_)
        m = jnp.mean(g, axis=(2, 3, 4), keepdims=True)
        s = jnp.var(g, axis=(2, 3, 4), keepdims=True)
        return ((g - m) / jnp.sqrt(s + eps)).reshape(v.shape)

    def _ln_c(v, eps=1e-06):
        m = jnp.mean(v, axis=1, keepdims=True)
        s = jnp.var(v, axis=1, keepdims=True)
        return (v - m) / jnp.sqrt(s + eps)

    def _ln_t(v, eps=1e-05):
        m = jnp.mean(v, axis=-1, keepdims=True)
        s = jnp.var(v, axis=-1, keepdims=True)
        return (v - m) / jnp.sqrt(s + eps)

    def _to_tokens(v):
        B_, C_, H_, W_ = v.shape
        return v.reshape(B_, C_, H_ * W_).transpose(0, 2, 1)

    def _from_tokens(t, like):
        B_, C_, H_, W_ = like.shape
        return t.transpose(0, 2, 1).reshape(B_, C_, H_, W_)
    x = x + _L0_conv_ref(_gn(x), L0_conv_w_off, L0_conv_b_off, L0_conv_w_conv)
    x = x + _L1_conv_ref(_gn(x), L1_conv_W, L1_conv_b)
    return x

_drawn_inputs = setup_inputs


def setup_inputs(seed=0):
    import zlib

    import numpy as np

    out = dict(_drawn_inputs(seed))
    spreads = {'L0_conv_b_off': (0.0, 0.1)}
    factors = {'L1_conv_b': 3.391}
    for name, (base, spread) in spreads.items():
        noise = np.random.default_rng([zlib.crc32(name.encode()), seed]).standard_normal(out[name].shape)
        drawn = base * np.exp(spread * noise) if base else spread * noise
        out[name] = jnp.asarray(drawn.astype(out[name].dtype))
    for name, factor in factors.items():
        out[name] = (out[name] * factor).astype(out[name].dtype)
    return out
```

```python
from contextlib import ExitStack

import numpy as np

import concourse.bass as bass
from concourse import mybir

F32 = mybir.dt.float32
ALU = mybir.AluOpType
ACT = mybir.ActivationFunctionType

B, C, H, W = 8, 64, 16, 16
N = H * W
TAPS = 9
PAIRS = B // 2
HALF = N // 2
TILES = 4
LOW = 5
BLOCKS = 2
ROWS = 8 * BLOCKS
PADR, PADC = H + 4, W + 2
BLOCK_ROWS = [2 + 8 * w for w in range(BLOCKS)]
SLOTS = TILES * TAPS * BLOCKS
GROUP = 4
GROUPS = SLOTS // GROUP
RING = 3
S_BUFS = 1
EPS_GN = 1e-5
EPS_NORM2 = 1e-8 ** 2
OFFC = 32
POOL_TILES = (2,)
DVE_GROUPS = (1, 4, 7, 10, 13, 16)


def constants():
    p = np.arange(128)
    ident = np.eye(128)
    average = (p[:, None] // 2 == p[None, :] // 2) * 0.5
    difference = average * np.where(p % 2, -1.0, 1.0)[:, None]
    ones = (p[:, None] // C == p[None, :] // C) * 1.0
    cy = np.stack([(8 * j + p[:, None] // W) - np.arange(ROWS) for j in range(2)], 1).reshape(128, -1)
    cx = (p[:, None] % W) - np.arange(W)
    power = np.full((128, 1), -0.5)
    return np.concatenate([ident, average, difference, ones, cy, cx, power], 1).astype(np.float32)


def build(nc, x, w_off, b_off, w_conv, w1, b1, consts, out):
    ctx = ExitStack()
    with ctx:
        def sb(name, shape):
            return ctx.enter_context(nc.sbuf_tensor(name, shape, F32))

        def sem(name):
            return ctx.enter_context(nc.semaphore(name))

        x_sb = sb("x_sb", [128, PAIRS, N])
        x1_sb = sb("x1_sb", [128, PAIRS, N])
        table = sb("table", [128, consts.shape[1]])
        woff_nat = sb("woff_nat", [27, 2, C * TAPS])
        wconv_nat = sb("wconv_nat", [C, LOW, 2, C])
        w1_nat = sb("w1_nat", [C, 2, C])
        boff_col = sb("boff_col", [128, 1])
        b1_col = sb("b1_col", [128, 1])
        woff_T = sb("woff_T", [128, TAPS, 2 * OFFC])
        wconv_T = sb("wconv_T", [128, LOW, C])
        w1_T = sb("w1_T", [128, 128])
        gpad = sb("gpad", [128, 2, PADR, PADC])
        grows = sb("grows", [128, 2, PADR, W])
        conv_sb = sb("conv_sb", [128, 128])
        hats = sb("hats", [128, 2, TILES * TAPS * (ROWS + W)])
        mask = sb("mask", [128, 2, TILES, TAPS])
        S = sb("S", [128, S_BUFS, TILES * TAPS, BLOCKS * 128])
        ST = sb("ST", [128, 2, TILES * TAPS, BLOCKS, 128])
        xT = sb("xT", [128, 2, len(BLOCK_ROWS), 128])
        sampled = sb("sampled", [128, 2, 2, LOW, N])
        g2 = sb("g2", [128, 2, N])
        g2_sq = sb("g2_sq", [128, N])
        inv_norm2 = sb("inv_norm2", [128, N])
        norm2 = sb("norm2", [128, N])
        t_scaled = sb("t_scaled", [128, N])
        tT = sb("tT", [128, 2, 128])
        sim = sb("sim", [128, 2, 2, N])
        sim2 = sb("sim2", [128, 2, 2, N])
        y_sb = sb("y_sb", [128, PAIRS, N])
        stats6 = sb("stats6", [128, 2, 6])
        mv = sb("mv", [128, 2, 2])
        gstat = sb("gstat", [128, 2, 3])
        var = sb("var", [128, 2, 1])
        rstd = sb("rstd", [128, 2, 1])
        shift = sb("shift", [128, 2, 1])

        ident = table[:, 0:128]
        average = table[:, 128:256]
        difference = table[:, 256:384]
        ones_block = table[:, 384:512]
        cy = table[:, 512:512 + 2 * ROWS].rearrange("p (j r) -> p j r", j=2)
        cx = table[:, 512 + 2 * ROWS:512 + 2 * ROWS + W]
        minus_half = table[:, 512 + 2 * ROWS + W:512 + 2 * ROWS + W + 1]

        ring = [ctx.enter_context(nc.psum_tensor(f"ring{i}", [128, 512], F32)) for i in range(RING)]
        samp_ps = ctx.enter_context(nc.psum_tensor("samp_ps", [128, 2, 512], F32))
        out_ps = ctx.enter_context(nc.psum_tensor("out_ps", [128, 512], F32))
        prep_ps = ctx.enter_context(nc.psum_tensor("prep_ps", [128, 512], F32))
        att_ps = ctx.enter_context(nc.psum_tensor("att_ps", [128, 512], F32))

        x_in = [sem(f"x_in{k}") for k in range(PAIRS)]
        table_in, woff_in, wrest_in, bias_in = sem("table_in"), sem("woff_in"), sem("wrest_in"), sem("bias_in")
        zeroed = sem("zeroed")
        w_turned, woff_ready, wrest_ready = sem("w_turned"), sem("woff_ready"), sem("wrest_ready")
        gn_own = [sem("gn1_own"), sem("gn2_own")]
        gn_mv = [sem("gn1_mv"), sem("gn2_mv")]
        gn_group = [sem("gn1_group"), sem("gn2_group")]
        gn_var = [sem("gn1_var"), sem("gn2_var")]
        gn_rstd = [sem("gn1_rstd"), sem("gn2_rstd")]
        gn_shift = [sem("gn1_shift"), sem("gn2_shift")]
        g_ready = [sem("g1_ready"), sem("g2_ready")]
        rows_ready, conv_done, conv_out, off_turned = sem("rows_ready"), sem("conv_done"), sem("conv_out"), sem("off_turned")
        dist_ready, mask_ready, abs_ready, hats_ready, hy_masked = (
            sem("dist_ready"), sem("mask_ready"), sem("abs_ready"), sem("hats_ready"), sem("hy_masked"))
        xT_done, xT_out = sem("xT_done"), sem("xT_out")
        S_dve, S_pool = sem("S_dve"), sem("S_pool")
        ring_full, ring_act, ring_dve = sem("ring_full"), sem("ring_act"), sem("ring_dve")
        samp_done, samp_out = sem("samp_done"), sem("samp_out")
        out_done, x1_ready = sem("out_done"), sem("x1_ready")
        sq_ready, norm_t_done, norm2_ready, inv_ready, t_ready = (
            sem("sq_ready"), sem("norm_t_done"), sem("norm2_ready"), sem("inv_ready"), sem("t_ready"))
        tT_done, tT_out = sem("tT_done"), sem("tT_out")
        sim2_ready, att_done, y_own, y_ready, stored = (
            sem("sim2_ready"), sem("att_done"), sem("y_own"), sem("y_ready"), sem("stored"))

        items = []

        def tile_of_group(g):
            return (GROUP * g + GROUP - 1) // (TAPS * BLOCKS)

        def last_group(tile):
            return ((tile + 1) * TAPS * BLOCKS - 1) // GROUP

        for k in range(PAIRS + 1):
            for tile in range(TILES):
                if k < PAIRS:
                    items += [("turn", k, g) for g in range(GROUPS) if tile_of_group(g) == tile]
                if tile == 2 and k >= 1:
                    items += [("sim", k - 1, 0), ("sim", k - 1, 1)]
        index = {item: i for i, item in enumerate(items)}
        by_dve = [item[0] == "turn" and item[2] in DVE_GROUPS for item in items]

        def emptied_by(engine_is_dve, i):
            return sum(1 for j in range(i + 1) if by_dve[j] == engine_is_dve)

        def wait_emptied(eng, i):
            eng.wait_ge(ring_dve if by_dve[i] else ring_act, emptied_by(by_dve[i], i))

        def wait_emptied_up_to(eng, i):
            for is_dve, s in ((False, ring_act), (True, ring_dve)):
                if emptied_by(is_dve, i):
                    eng.wait_ge(s, emptied_by(is_dve, i))

        def S_count(k, tile, on_pool):
            return sum(1 for n in range(TILES * k + tile + 1) if (n % TILES in POOL_TILES) == on_pool)

        def S_part(k, tile):
            hy = hats[:, k % 2, 0:TILES * TAPS * ROWS].rearrange("p (s r) -> p s r", r=ROWS)
            hx = hats[:, k % 2, TILES * TAPS * ROWS:].rearrange("p (s c) -> p s c", c=W)
            s = slice(TAPS * tile, TAPS * tile + TAPS)
            return (S[:, k % S_BUFS, s, :].rearrange("p s (r c) -> p s r c", c=W),
                    hy[:, s, :].unsqueeze(3).to_broadcast([128, TAPS, ROWS, W]),
                    hx[:, s, :].unsqueeze(2).to_broadcast([128, TAPS, ROWS, W]))

        def image(k):
            return gpad[:, k % 2, 2:2 + H, 1:1 + W]

        block = ctx.enter_context(nc.Block())

        @block.sync
        def _(sp):
            pair = lambda a, k: a[2 * k:2 * k + 2].rearrange("b c h w -> (b c) (h w)")
            sp.dma_start(x_sb[:, 0, :], pair(x, 0)).then_inc(x_in[0], 16)
            sp.dma_start(table[:], consts).then_inc(table_in, 16)
            for k in range(1, PAIRS):
                sp.dma_start(x_sb[:, k, :], pair(x, k)).then_inc(x_in[k], 16)
            for k in range(PAIRS):
                sp.wait_ge(y_ready, k + 1)
                sp.dma_start(pair(out, k), y_sb[:, k, :]).then_inc(stored, 16)
            sp.wait_ge(stored, 16 * PAIRS)

        @block.gpsimd
        def _(pool):
            nc.gpsimd.memset(boff_col[:], 0.0).then_inc(zeroed, 1)
            nc.gpsimd.memset(woff_T[:], 0.0).then_inc(zeroed, 1)
            nc.gpsimd.memset(gpad[:], 0.0).then_inc(zeroed, 1)
            nc.gpsimd.memset(grows[:], 0.0).then_inc(zeroed, 1)
            nc.gpsimd.memset(wconv_T[:, 0, :], 0.0).then_inc(zeroed, 1)
            nc.gpsimd.memset(w1_T[:], 0.0).then_inc(zeroed, 1)

            def power(i, k):
                pool.wait_ge(gn_var[i], k + 1)
                if i == 0 and k >= 1:
                    pool.wait_ge(rows_ready, k)
                if i == 0 and k == 0:
                    pool.wait_ge(table_in, 16)
                nc.gpsimd.tensor_tensor(rstd[:, i, :], var[:, i, :], minus_half, ALU.pow).then_inc(gn_rstd[i], 1)

            def multiply(k, tile):
                pool.wait_ge(hy_masked, k + 1)
                if k >= S_BUFS:
                    pool.wait_ge(ring_full, index["turn", k - S_BUFS, last_group(tile)] + 1)
                o, a, b = S_part(k, tile)
                nc.gpsimd.tensor_tensor(o, a, b, ALU.mult).then_inc(S_pool, 1)

            def square(k):
                for b in range(2):
                    wait_emptied(pool, index["sim", k, b])
                    if k >= 1:
                        pool.wait_ge(att_done, k)
                    nc.gpsimd.tensor_tensor(sim2[:, b], sim[:, b], sim[:, b], ALU.mult).then_inc(sim2_ready, 1)

            power(0, 0)
            for k in range(PAIRS + 1):
                for tile in range(TILES):
                    if k < PAIRS and tile in POOL_TILES:
                        multiply(k, tile)
                    if tile == 0 and k + 1 < PAIRS:
                        power(0, k + 1)
                    if tile == 0 and k >= 1:
                        power(1, k - 1)
                    if tile == 2 and k >= 1:
                        square(k - 1)

        @block.tensor
        def _(pe):
            def turn_weights():
                pe.wait_ge(table_in, 16)
                pe.wait_ge(woff_in, 32)
                for t in range(TAPS):
                    mm = pe.transpose(att_ps[:, OFFC * t:OFFC * t + 27], woff_nat[:, :, t:C * TAPS:TAPS], ident[0:27, 0:27])
                mm.then_inc(w_turned, 1)
                pe.wait_ge(wrest_in, 64)
                for t in range(LOW):
                    pe.transpose(samp_ps[:, 0, C * t:C * t + C], wconv_nat[:, t, :, :].rearrange("o h c -> o (h c)"), ident[0:C, 0:C])
                pe.transpose(samp_ps[:, 0, C * LOW:C * LOW + C], w1_nat[:].rearrange("o h c -> o (h c)"), ident[0:C, 0:C]).then_inc(w_turned, 1)

            def group_means(i, k):
                pe.wait_ge(gn_mv[i], k + 1)
                ps = prep_ps if i == 0 else att_ps
                if i == 0 and k >= 1:
                    pe.wait_ge(xT_out, k)
                if i == 1 and k == 0:
                    pe.wait_ge(woff_ready, 2)
                if i == 1 and k >= 1:
                    pe.wait_ge(y_own, k)
                pe.matmul(ps[:, 0:2], average, mv[:, i, :], start=True, stop=True)
                pe.matmul(ps[:, 2:3], difference, mv[:, i, 0:1], start=True, stop=True).then_inc(gn_group[i], 1)

            def convolve(k):
                pe.wait_ge(g_ready[0], k + 1)
                if k == 0:
                    pe.wait_ge(woff_ready, 2)
                for t in range(TAPS):
                    for j in range(2):
                        r, c = 8 * j + 1 + t // 3, t % 3
                        mm = pe.matmul(prep_ps[64 * j:64 * j + 64, 0:HALF], woff_T[:, t, :],
                                       gpad[:, k % 2, r:r + 8, c:c + W], start=(t == 0), stop=(t == TAPS - 1))
                mm.then_inc(conv_done, 1)

            def turn_offsets(k):
                pe.wait_ge(conv_out, k + 1)
                pe.transpose(prep_ps[:, 128:256], conv_sb[:], ident).then_inc(off_turned, 1)

            def turn_image(k):
                pe.wait_ge(mask_ready, k + 1)
                pe.wait_ge(rows_ready, k + 1)
                for w, r in enumerate(BLOCK_ROWS):
                    mm = pe.transpose(prep_ps[:, 128 * w:128 * w + 128],
                                      grows[:, k % 2, r:r + 8, :].rearrange("p r c -> p (r c)"), ident)
                mm.then_inc(xT_done, 1)

            def turn(k, tile):
                for g in range(GROUPS):
                    if tile_of_group(g) != tile:
                        continue
                    i = index["turn", k, g]
                    pe.wait_ge(S_pool if tile in POOL_TILES else S_dve, S_count(k, tile, tile in POOL_TILES))
                    if i >= RING:
                        wait_emptied(pe, i - RING)
                    for n in range(GROUP):
                        s, w = divmod(GROUP * g + n, BLOCKS)
                        mm = pe.transpose(ring[i % RING][:, 128 * n:128 * n + 128],
                                          S[:, k % S_BUFS, s, 128 * w:128 * w + 128], ident)
                    mm.then_inc(ring_full, 1)

            def sample(k, tile):
                j, b = divmod(tile, 2)
                wait_emptied_up_to(pe, index["turn", k, last_group(tile)])
                pe.wait_ge(xT_out, k + 1)
                if k == 0 and tile == 0:
                    pe.wait_ge(wrest_ready, 1)
                if TILES * k + tile >= 1:
                    pe.wait_ge(samp_out, TILES * k + tile)
                for a in range(2):
                    for w in range(BLOCKS):
                        for h in range(2):
                            s = TAPS * tile + (LOW - 1) * h
                            mm = pe.matmul(samp_ps[64 * h:64 * h + 64, a, 0:LOW * 64], xT[:, k % 2, w, C * b:C * b + C],
                                           ST[:, k % 2, s:s + LOW, w, 64 * a:64 * a + 64],
                                           start=(w == 0), stop=(w == BLOCKS - 1))
                mm.then_inc(samp_done, 1)

            def project(k):
                pe.wait_ge(samp_out, TILES * (k + 1))
                if k >= 1:
                    pe.wait_ge(x1_ready, k)
                for t in range(LOW):
                    for b in range(2):
                        mm = pe.matmul(out_ps[64 * b:64 * b + 64, 0:N], wconv_T[:, t, :], sampled[:, k % 2, b, t, :],
                                       start=(t == 0), stop=(t == LOW - 1))
                mm.then_inc(out_done, 1)

            def norms_and_t(k):
                pe.wait_ge(g_ready[1], k + 1)
                pe.matmul(att_ps[:, N:2 * N], w1_T[:], g2[:, k % 2, :], start=True, stop=True)
                pe.wait_ge(sq_ready, k + 1)
                pe.matmul(att_ps[:, 0:N], ones_block, g2_sq[:], start=True, stop=True).then_inc(norm_t_done, 1)

            def turn_t(k):
                pe.wait_ge(t_ready, k + 1)
                for m in range(2):
                    mm = pe.transpose(att_ps[:, 128 * m:128 * m + 128], t_scaled[:, 128 * m:128 * m + 128], ident)
                mm.then_inc(tT_done, 1)

            def similarities(k):
                for b in range(2):
                    i = index["sim", k, b]
                    wait_emptied(pe, i - RING)
                    for m in range(2):
                        g = g2[64 * b:64 * b + 64, k % 2, :]
                        mm = pe.matmul(ring[i % RING][:, N * m:N * m + N], g[:, 128 * m:128 * m + 128], g,
                                       start=True, stop=True)
                    mm.then_inc(ring_full, 1)

            def attend(k):
                pe.wait_ge(tT_out, k + 1)
                pe.wait_ge(sim2_ready, 2 * k + 2)
                for m in range(2):
                    for b in range(2):
                        mm = pe.matmul(att_ps[64 * b:64 * b + 64, N:2 * N], tT[:, m, 64 * b:64 * b + 64],
                                       sim2[:, b, m, :], start=(m == 0), stop=(m == 1))
                mm.then_inc(att_done, 1)

            turn_weights()
            group_means(0, 0)
            convolve(0)
            turn_offsets(0)
            turn_image(0)
            for k in range(PAIRS + 1):
                for tile in range(TILES):
                    if k < PAIRS:
                        turn(k, tile)
                    if tile == 0:
                        if k + 1 < PAIRS:
                            group_means(0, k + 1)
                        if k >= 1:
                            group_means(1, k - 1)
                    if tile == 1:
                        if k + 1 < PAIRS:
                            convolve(k + 1)
                        if k >= 1:
                            norms_and_t(k - 1)
                    if tile == 2:
                        if k + 1 < PAIRS:
                            turn_offsets(k + 1)
                        if k >= 1:
                            turn_t(k - 1)
                            similarities(k - 1)
                    if tile == 3:
                        if k + 1 < PAIRS:
                            turn_image(k + 1)
                        if k >= 1:
                            attend(k - 1)
                    if k < PAIRS and tile >= 1:
                        sample(k, tile - 1)
                if k < PAIRS:
                    sample(k, TILES - 1)
                    project(k)

        @block.scalar
        def _(act):
            for h in range(2):
                act.dma_start(woff_nat[:, h, :], w_off.rearrange("o c a b -> o (c a b)")).then_inc(woff_in, 16)
            act.wait_ge(zeroed, 1)
            for g in range(4):
                act.dma_start(boff_col[OFFC * g:OFFC * g + 27, :], b_off.rearrange("(a b) -> a b", b=1)).then_inc(bias_in, 16)
            for h in range(2):
                first = (LOW - 1) * h * C
                act.dma_start(wconv_nat[:, :, h, :],
                              w_conv[:, first:first + LOW * C].rearrange("o (t c) -> o t c", c=C)).then_inc(wrest_in, 16)
                act.dma_start(w1_nat[:, h, :], w1).then_inc(wrest_in, 16)
                act.dma_start(b1_col[C * h:C * h + C, :], b1.rearrange("(a b) -> a b", b=1)).then_inc(bias_in, 16)
            act.wait_ge(w_turned, 1)
            act.wait_ge(zeroed, 2)
            turned = att_ps[64:128, 0:TAPS * OFFC].rearrange("p (t o) -> p t o", o=OFFC)[:, :, 0:27]
            nc.scalar.copy(woff_T[64:128, :, OFFC:OFFC + 27], turned).then_inc(woff_ready, 1)

            def normalised_rows(k):
                act.wait_ge(gn_shift[0], k + 1)
                if k == 0:
                    act.wait_ge(zeroed, 4)
                if k >= 2:
                    act.wait_ge(xT_done, k - 1)
                nc.scalar.activation(grows[:, k % 2, 2:2 + H, :].rearrange("p r c -> p (r c)"), x_sb[:, k, :], ACT.Identity,
                                     bias=shift[:, 0, 0:1], scale=rstd[:, 0, 0:1]).then_inc(rows_ready, 1)

            def conv_bias(k):
                act.wait_ge(conv_done, k + 1)
                if k == 0:
                    act.wait_ge(bias_in, 96)
                if k >= 1:
                    act.wait_ge(off_turned, k)
                nc.scalar.activation(conv_sb[:], prep_ps[:, 0:HALF], ACT.Identity, bias=boff_col[:, 0:1]).then_inc(conv_out, 1)

            def make_hats(k):
                act.wait_ge(dist_ready, 3 * (k + 1))
                offs = prep_ps[:, 128:256].rearrange("p (t o) -> p t o", o=OFFC)
                nc.scalar.activation(mask[:, k % 2], offs[:, :, 2 * TAPS:3 * TAPS], ACT.Sigmoid).then_inc(mask_ready, 1)
                h = hats[:, k % 2, :]
                nc.scalar.activation(h, h, ACT.Abs).then_inc(abs_ready, 1)
                act.wait_ge(abs_ready, k + 1)
                nc.scalar.activation(h, h, ACT.Relu, scale=-1.0, bias=1.0).then_inc(hats_ready, 1)

            def image_out(k):
                act.wait_ge(xT_done, k + 1)
                if k >= 2:
                    act.wait_ge(samp_done, TILES * (k - 1))
                n = len(BLOCK_ROWS) * 128
                nc.scalar.copy(xT[:, k % 2].rearrange("p w c -> p (w c)"), prep_ps[:, 0:n]).then_inc(xT_out, 1)

            def groups_out(k, tile):
                for g in range(GROUPS):
                    if tile_of_group(g) != tile or g in DVE_GROUPS:
                        continue
                    i = index["turn", k, g]
                    act.wait_ge(ring_full, i + 1)
                    if k >= 2:
                        act.wait_ge(samp_done, TILES * (k - 1))
                    dst = ST[:, k % 2].rearrange("p s w q -> p (s w q)")[:, 512 * g:512 * g + 512]
                    nc.scalar.copy(dst, ring[i % RING][:]).then_inc(ring_act, 1)

            def sampled_out(k, tile):
                j, b = divmod(tile, 2)
                act.wait_ge(samp_done, TILES * k + tile + 1)
                if k >= 2:
                    act.wait_ge(out_done, k - 1)
                dst = sampled[:, k % 2, b, :, HALF * j:HALF * j + HALF].rearrange("p t (a q) -> p a t q", a=2)
                src = samp_ps[:, :, 0:LOW * 64].rearrange("p a (t q) -> p a t q", t=LOW)
                nc.scalar.copy(dst, src).then_inc(samp_out, 1)

            def squares(k):
                act.wait_ge(g_ready[1], k + 1)
                if k >= 1:
                    act.wait_ge(norm_t_done, k)
                nc.scalar.activation(g2_sq[:], g2[:, k % 2, :], ACT.Square).then_inc(sq_ready, 1)

            def t_out(k):
                act.wait_ge(tT_done, k + 1)
                if k >= 1:
                    act.wait_ge(att_done, k)
                nc.scalar.copy(tT[:].rearrange("p m c -> p (m c)"), att_ps[:, 0:N]).then_inc(tT_out, 1)

            def relu_similarities(k):
                for b in range(2):
                    i = index["sim", k, b]
                    act.wait_ge(ring_full, i + 1)
                    if k >= 1:
                        act.wait_ge(sim2_ready, 2 * k)
                    nc.scalar.activation(sim[:, b].rearrange("p m n -> p (m n)"), ring[i % RING][:], ACT.Relu).then_inc(ring_act, 1)

            normalised_rows(0)
            conv_bias(0)
            make_hats(0)
            image_out(0)
            for k in range(PAIRS + 1):
                for tile in range(TILES):
                    if k < PAIRS:
                        groups_out(k, tile)
                    if tile == 1:
                        if k + 1 < PAIRS:
                            normalised_rows(k + 1)
                            conv_bias(k + 1)
                        if k >= 1:
                            squares(k - 1)
                    if tile == 2:
                        if k + 1 < PAIRS:
                            make_hats(k + 1)
                        if k >= 1:
                            t_out(k - 1)
                            relu_similarities(k - 1)
                    if tile == 3:
                        if k + 1 < PAIRS:
                            image_out(k + 1)
                    if k < PAIRS and tile >= 1:
                        sampled_out(k, tile - 1)
                if k < PAIRS:
                    sampled_out(k, TILES - 1)

        @block.vector
        def _(dve):
            def statistics(i, k):
                if i == 0:
                    dve.wait_ge(x_in[k], 16)
                else:
                    dve.wait_ge(x1_ready, k + 1)
                src = (x_sb if i == 0 else x1_sb)[:, k, :]
                nc.vector.bn_stats(stats6[:, i, :], src).then_inc(gn_own[i], 1)
                dve.wait_ge(gn_own[i], 3 * k + 1)
                nc.vector.bn_aggr(mv[:, i, :], stats6[:, i, :]).then_inc(gn_mv[i], 1)

            def group_variance(i, k):
                ps = prep_ps if i == 0 else att_ps
                dve.wait_ge(gn_group[i], k + 1)
                nc.vector.tensor_copy(gstat[:, i, :], ps[:, 0:3]).then_inc(gn_own[i], 1)
                dve.wait_ge(gn_own[i], 3 * k + 2)
                nc.vector.scalar_tensor_tensor(out=var[:, i, :], in0=gstat[:, i, 2:3], scalar=gstat[:, i, 2:3],
                                               in1=gstat[:, i, 1:2], op0=ALU.mult, op1=ALU.add).then_inc(gn_own[i], 1)
                dve.wait_ge(gn_own[i], 3 * k + 3)
                nc.vector.tensor_scalar(var[:, i, :], var[:, i, :], EPS_GN, None, ALU.add).then_inc(gn_var[i], 1)

            def normalise(i, k):
                dve.wait_ge(gn_rstd[i], k + 1)
                nc.vector.scalar_tensor_tensor(out=shift[:, i, :], in0=gstat[:, i, 0:1], scalar=-1.0,
                                               in1=rstd[:, i, :], op0=ALU.mult, op1=ALU.mult).then_inc(gn_shift[i], 1)
                dve.wait_ge(gn_shift[i], k + 1)
                if i == 0:
                    src, dst = x_sb[:, k, :].rearrange("p (h w) -> p h w", w=W), image(k)
                    if k == 0:
                        dve.wait_ge(zeroed, 3)
                    if k >= 2:
                        dve.wait_ge(xT_done, k - 1)
                else:
                    src, dst = x1_sb[:, k, :], g2[:, k % 2, :]
                nc.vector.tensor_scalar(dst, src, rstd[:, i, 0:1], shift[:, i, 0:1], ALU.mult, ALU.add).then_inc(g_ready[i], 1)

            def distances(k):
                dve.wait_ge(off_turned, k + 1)
                if k >= 2:
                    dve.wait_ge(S_pool, S_count(k - 2, TILES - 1, True))
                    dve.wait_ge(S_dve, S_count(k - 2, TILES - 1, False))
                offs = prep_ps[:, 128:256].rearrange("p (t o) -> p t o", o=OFFC)
                ty = hats[:, k % 2, 0:TILES * TAPS * ROWS].rearrange("p (t s r) -> p t s r", t=TILES, r=ROWS)
                tx = hats[:, k % 2, TILES * TAPS * ROWS:].rearrange("p (t s c) -> p t s c", t=TILES, c=W)
                for j in range(2):
                    nc.vector.tensor_tensor(ty[:, 2 * j:2 * j + 2],
                                            offs[:, 2 * j:2 * j + 2, 0:TAPS].unsqueeze(3).to_broadcast([128, 2, TAPS, ROWS]),
                                            cy[:, j, :].unsqueeze(1).unsqueeze(1).to_broadcast([128, 2, TAPS, ROWS]),
                                            ALU.add).then_inc(dist_ready, 1)
                nc.vector.tensor_tensor(tx, offs[:, :, TAPS:2 * TAPS].unsqueeze(3).to_broadcast([128, TILES, TAPS, W]),
                                        cx.unsqueeze(1).unsqueeze(1).to_broadcast([128, TILES, TAPS, W]),
                                        ALU.add).then_inc(dist_ready, 1)

            def mask_rows(k):
                dve.wait_ge(hats_ready, k + 1)
                hy = hats[:, k % 2, 0:TILES * TAPS * ROWS].rearrange("p (s r) -> p s r", r=ROWS)
                m = mask[:, k % 2].rearrange("p t s -> p (t s)").unsqueeze(2).to_broadcast([128, TILES * TAPS, ROWS])
                nc.vector.tensor_tensor(hy, hy, m, ALU.mult).then_inc(hy_masked, 1)

            def multiply(k, tile):
                dve.wait_ge(hy_masked, k + 1)
                if k >= S_BUFS:
                    dve.wait_ge(ring_full, index["turn", k - S_BUFS, last_group(tile)] + 1)
                o, a, b = S_part(k, tile)
                nc.vector.tensor_tensor(o, a, b, ALU.mult).then_inc(S_dve, 1)

            def groups_out(k, tile):
                for g in range(GROUPS):
                    if tile_of_group(g) != tile or g not in DVE_GROUPS:
                        continue
                    i = index["turn", k, g]
                    dve.wait_ge(ring_full, i + 1)
                    if k >= 2:
                        dve.wait_ge(samp_done, TILES * (k - 1))
                    dst = ST[:, k % 2].rearrange("p s w q -> p (s w q)")[:, 512 * g:512 * g + 512]
                    nc.vector.tensor_copy(dst, ring[i % RING][:]).then_inc(ring_dve, 1)

            def residual(k):
                dve.wait_ge(out_done, k + 1)
                nc.vector.tensor_tensor(x1_sb[:, k, :], out_ps[:, 0:N], x_sb[:, k, :], ALU.add).then_inc(x1_ready, 1)

            def scale_t(k):
                dve.wait_ge(norm_t_done, k + 1)
                if k >= 1:
                    dve.wait_ge(y_own, k)
                nc.vector.tensor_scalar(norm2[:], att_ps[:, 0:N], EPS_NORM2, None, ALU.max).then_inc(norm2_ready, 1)
                dve.wait_ge(norm2_ready, k + 1)
                nc.vector.reciprocal(inv_norm2[:], norm2[:]).then_inc(inv_ready, 1)
                dve.wait_ge(inv_ready, k + 1)
                if k == 0:
                    dve.wait_ge(bias_in, 96)
                if k >= 1:
                    dve.wait_ge(tT_done, k)
                nc.vector.scalar_tensor_tensor(out=t_scaled[:], in0=att_ps[:, N:2 * N], scalar=b1_col[:, 0:1],
                                               in1=inv_norm2[:], op0=ALU.add, op1=ALU.mult).then_inc(t_ready, 1)

            def finish(k):
                dve.wait_ge(att_done, k + 1)
                y = y_sb[:, k, :]
                nc.vector.tensor_tensor(y, att_ps[:, N:2 * N], inv_norm2[:], ALU.mult).then_inc(y_own, 1)
                dve.wait_ge(y_own, k + 1)
                nc.vector.tensor_tensor(y, y, x1_sb[:, k, :], ALU.add).then_inc(y_ready, 1)

            statistics(0, 0)
            group_variance(0, 0)
            normalise(0, 0)
            dve.wait_ge(w_turned, 1)
            dve.wait_ge(zeroed, 6)
            turned = att_ps[0:64, 0:TAPS * OFFC].rearrange("p (t o) -> p t o", o=OFFC)[:, :, 0:27]
            nc.vector.tensor_copy(woff_T[0:64, :, 0:27], turned).then_inc(woff_ready, 1)
            dve.wait_ge(w_turned, 2)
            nc.vector.tensor_copy(wconv_T[:, 1:LOW, :], samp_ps[:, 0, C:C * LOW].rearrange("p (t o) -> p t o", o=C))
            nc.vector.tensor_copy(wconv_T[0:64, 0, :], samp_ps[0:64, 0, 0:C])
            nc.vector.tensor_copy(w1_T[0:64, 0:64], samp_ps[0:64, 0, C * LOW:C * LOW + C])
            nc.vector.tensor_copy(w1_T[64:128, 64:128], samp_ps[64:128, 0, C * LOW:C * LOW + C]).then_inc(wrest_ready, 1)
            distances(0)
            mask_rows(0)
            for k in range(PAIRS + 1):
                for tile in range(TILES):
                    if tile == 0:
                        if k + 1 < PAIRS:
                            statistics(0, k + 1)
                        if k >= 1:
                            statistics(1, k - 1)
                    if k < PAIRS and tile not in POOL_TILES:
                        multiply(k, tile)
                    if tile == 0:
                        if k + 1 < PAIRS:
                            group_variance(0, k + 1)
                        if k >= 1:
                            group_variance(1, k - 1)
                    if k < PAIRS:
                        groups_out(k, tile)
                    if tile == 0:
                        if k + 1 < PAIRS:
                            normalise(0, k + 1)
                        if k >= 1:
                            normalise(1, k - 1)
                    if tile == 1 and k >= 1:
                        scale_t(k - 1)
                    if tile == 2 and k + 1 < PAIRS:
                        distances(k + 1)
                    if tile == 3:
                        if k + 1 < PAIRS:
                            mask_rows(k + 1)
                        if k >= 1:
                            finish(k - 1)
                if k < PAIRS:
                    residual(k)


def kernel(x, L0_conv_w_off, L0_conv_b_off, L0_conv_w_conv, L1_conv_W, L1_conv_b):
    import concourse.bacc as bacc
    from concourse.bass_utils import run_bass_kernel_spmd

    nc = bacc.Bacc("TRN2", target_bir_lowering=False, num_devices=1)
    given = {"x": x, "w_off": L0_conv_w_off, "b_off": L0_conv_b_off, "w_conv": L0_conv_w_conv,
             "w1": L1_conv_W, "b1": L1_conv_b, "consts": constants()}
    arrays = {name: np.ascontiguousarray(a) for name, a in given.items()}
    args = [nc.dram_tensor(name, a.shape, mybir.dt.from_np(a.dtype), kind="ExternalInput").ap()
            for name, a in arrays.items()]
    out = nc.dram_tensor("out", (B, C, H, W), F32, kind="ExternalOutput").ap()
    build(nc, *args, out)
    result = run_bass_kernel_spmd(nc, [arrays], core_ids=[0])
    return result.results[0]["out"]
```

```python
from contextlib import ExitStack

import numpy as np

import concourse.bass as bass
from concourse import mybir

F32 = mybir.dt.float32
ALU = mybir.AluOpType
ACT = mybir.ActivationFunctionType
AX = mybir.AxisListType

B, C, H, W = 8, 64, 16, 16
N = H * W
TAPS = 9
PAIRS = B // 2
HALF = N // 2
TILES = 4
LOW = 5
PADR, PADC = H + 4, W + 2
GROUP = 4
RING = 3
REACH = 2
EPS_GN = 1e-5
EPS_NORM2 = 1e-8 ** 2
OFFC = 32


def constants():
    p = np.arange(128)
    ident = np.eye(128)
    average = (p[:, None] // 2 == p[None, :] // 2) * 0.5
    ones = (p[:, None] // C == p[None, :] // C) * 1.0
    row = p[:, None] // W
    cy = np.concatenate([8 * j + row - np.arange(H) for j in range(2)], 1)
    cy_window = row % 4 + REACH - np.arange(8)
    cx = (p[:, None] % W) - np.arange(W)
    power = np.full((128, PAIRS), -0.5)
    return np.concatenate([ident, average, power, ones, cy, cy_window, cx], 1).astype(np.float32)


def run_pairs(nc, general, far, x, w_off, b_off, w_conv, w1, b1, consts, out):
    BLOCKS = 2 if general else 1
    ROWS = 8 * BLOCKS
    BLOCK_ROWS = [2, 10] if general else [0, 4, 8, 12]
    SLOTS = TILES * TAPS * BLOCKS
    GROUPS = SLOTS // GROUP
    S_BUFS = 1 if general else 2
    POOL_TILE = 2
    DVE_GROUPS = (1, 4, 7, 10, 13, 16) if general else (7,)

    way = "general_" if general else ""
    ctx = ExitStack()
    with ctx:
        def sb(name, shape):
            return ctx.enter_context(nc.sbuf_tensor(way + name, shape, F32))

        def sem(name):
            return ctx.enter_context(nc.semaphore(way + name))

        x_sb = sb("x_sb", [128, PAIRS, N])
        x1_sb = sb("x1_sb", [128, PAIRS, N])
        table = sb("table", [128, consts.shape[1]])
        woff_nat = sb("woff_nat", [27, 2, C * TAPS])
        wconv_nat = sb("wconv_nat", [C, LOW, 2, C])
        w1_nat = sb("w1_nat", [C, 2, C])
        boff_col = sb("boff_col", [128, 1])
        b1_col = sb("b1_col", [128, 1])
        woff_T = sb("woff_T", [128, TAPS, 2 * OFFC])
        wconv_T = sb("wconv_T", [128, LOW, C])
        w1_T = sb("w1_T", [128, 128])
        gpad = sb("gpad", [128, 2, PADR, PADC])
        grows = sb("grows", [128, 2, PADR, W])
        conv_sb = sb("conv_sb", [128, 128])
        hats = sb("hats", [128, 2, 2, 2 * TAPS * (ROWS + W)])
        mask = sb("mask", [128, 2, TILES, TAPS])
        S = sb("S", [128, S_BUFS, TILES * TAPS, BLOCKS * 128])
        ST = sb("ST", [128, 2, TILES * TAPS, BLOCKS, 128])
        xT = sb("xT", [128, 2, len(BLOCK_ROWS), 128])
        sampled = sb("sampled", [128, 2, 2, LOW, N])
        g2 = sb("g2", [128, 2, N])
        g2_sq = sb("g2_sq", [128, N])
        inv_norm2 = sb("inv_norm2", [128, N])
        norm2 = sb("norm2", [128, N])
        t_scaled = sb("t_scaled", [128, N])
        tT = sb("tT", [128, 2, 128])
        sim = sb("sim", [128, 2, 2, N])
        sim2 = sb("sim2", [128, 2, 2, N])
        y_sb = sb("y_sb", [128, PAIRS, N])
        stats6 = sb("stats6", [128, 2, PAIRS, 6])
        mv = sb("mv", [128, 2, PAIRS, 2])
        gmv = sb("gmv", [128, 2, PAIRS, 2])
        gdiff = sb("gdiff", [128, 2, PAIRS])
        var = sb("var", [128, 2, PAIRS])
        rstd = sb("rstd", [128, 2, PAIRS])
        shift = sb("shift", [128, 2, PAIRS])
        warm = sb("warm", [128, 1])
        warm_w = ctx.enter_context(nc.sbuf_tensor(way + "warm_w", [128, N], mybir.dt.bfloat16))

        reach = sb("reach", [128, PAIRS + 2])
        ident = table[:, 0:128]
        average = table[:, 128:256]
        minus_half = table[:, 256:256 + PAIRS]
        early = 256 + PAIRS
        ones_block = table[:, early:early + 128]
        late = table[:, early + 128:]
        cy = late[:, 0:32].rearrange("p (j r) -> p j r", j=2)
        cy_window = late[:, 32:40]
        cx = late[:, 40:40 + W]

        ring = [ctx.enter_context(nc.psum_tensor(way + f"ring{i}", [128, 512], F32)) for i in range(RING)]
        samp_ps = ctx.enter_context(nc.psum_tensor(way + "samp_ps", [128, 2, 512], F32))
        out_ps = ctx.enter_context(nc.psum_tensor(way + "out_ps", [128, 512], F32))
        prep_ps = ctx.enter_context(nc.psum_tensor(way + "prep_ps", [128, 512], F32))
        att_ps = ctx.enter_context(nc.psum_tensor(way + "att_ps", [128, 512], F32))

        x_in = [sem(f"x_in{k}") for k in range(PAIRS)]
        table_in, table_rest_in, woff_in, wrest_in, bias_in, b1_in = sem("table_in"), sem("table_rest_in"), sem("woff_in"), sem("wrest_in"), sem("bias_in"), sem("b1_in")
        zeroed, warm_zeroed = sem("zeroed"), sem("warm_zeroed")
        w_turned, woff_ready, wrest_ready = sem("w_turned"), sem("woff_ready"), sem("wrest_ready")
        gn_own = [sem("gn1_own"), sem("gn2_own")]
        gn_mv = [sem("gn1_mv"), sem("gn2_mv")]
        gn_group = [sem("gn1_group"), sem("gn2_group")]
        gn_var = [sem("gn1_var"), sem("gn2_var")]
        gn_rstd = [sem("gn1_rstd"), sem("gn2_rstd")]
        gn_shift = [sem("gn1_shift"), sem("gn2_shift")]
        g_ready = [sem("g1_ready"), sem("g2_ready")]
        rows_ready, conv_done, conv_out, off_turned = sem("rows_ready"), sem("conv_done"), sem("conv_out"), sem("off_turned")
        dist_ready, mask_ready, abs_ready, hats_ready, hy_masked = (
            sem("dist_ready"), sem("mask_ready"), sem("abs_ready"), sem("hats_ready"), sem("hy_masked"))
        xT_done, xT_out = sem("xT_done"), sem("xT_out")
        S_dve, S_pool = sem("S_dve"), sem("S_pool")
        ring_full, ring_act, ring_dve = sem("ring_full"), sem("ring_act"), sem("ring_dve")
        samp_done, samp_out = sem("samp_done"), sem("samp_out")
        out_done, x1_ready = sem("out_done"), sem("x1_ready")
        sq_ready, norm_t_done, norm2_ready, inv_ready, t_ready = (
            sem("sq_ready"), sem("norm_t_done"), sem("norm2_ready"), sem("inv_ready"), sem("t_ready"))
        tT_done, tT_out = sem("tT_done"), sem("tT_out")
        sim2_ready, sim2_last, att_done, y_own, y_ready, stored = (
            sem("sim2_ready"), sem("sim2_last"), sem("att_done"), sem("y_own"), sem("y_ready"), sem("stored"))

        reach_own, reach_ready, reach_turned, far_set = sem("reach_own"), sem("reach_ready"), sem("reach_turned"), sem("far_set")

        GN1_FIRST, GN1_REST = (0, 0, 0, 1), (0, 1, 1, PAIRS)

        def gn2(k):
            return (1, k, k, k + 1)

        def group_ps(part):
            ps, n = (prep_ps if part == GN1_FIRST else att_ps), part[3] - part[2]
            return ps[:, 0:2 * n].rearrange("p (k s) -> p k s", s=2)

        items = []

        def tile_of_group(g):
            return (GROUP * g + GROUP - 1) // (TAPS * BLOCKS)

        def last_group(tile):
            return ((tile + 1) * TAPS * BLOCKS - 1) // GROUP

        for k in range(PAIRS + 1):
            for tile in range(TILES):
                if k < PAIRS:
                    items += [("turn", k, g) for g in range(GROUPS) if tile_of_group(g) == tile]
                if tile == 3 and k >= 1:
                    items += [("sim", k - 1, 0), ("sim", k - 1, 1)]
        index = {item: i for i, item in enumerate(items)}
        by_dve = [item[0] == "turn" and item[2] in DVE_GROUPS for item in items]

        def emptied_by(engine_is_dve, i):
            return sum(1 for j in range(i + 1) if by_dve[j] == engine_is_dve)

        def wait_emptied(eng, i):
            eng.wait_ge(ring_dve if by_dve[i] else ring_act, emptied_by(by_dve[i], i))

        def wait_emptied_up_to(eng, i):
            for is_dve, s in ((False, ring_act), (True, ring_dve)):
                if emptied_by(is_dve, i):
                    eng.wait_ge(s, emptied_by(is_dve, i))

        def S_count(k, tile, on_pool):
            return sum(1 for n in range(TILES * k + tile + 1) if (n % TILES == POOL_TILE) == on_pool)

        def hats_of(k, j):
            h = hats[:, k % 2, j, :]
            return (h[:, 0:2 * TAPS * ROWS].rearrange("p (s r) -> p s r", r=ROWS),
                    h[:, 2 * TAPS * ROWS:].rearrange("p (s c) -> p s c", c=W))

        def halves(k):
            return [(0,), (1,)] if k == 0 else [(0, 1)]

        def hats_count(k, j):
            return j + 1 if k == 0 else k + 2

        def S_part(k, tile):
            hy, hx = hats_of(k, tile // 2)
            s, of_s = slice(TAPS * (tile % 2), TAPS * (tile % 2) + TAPS), slice(TAPS * tile, TAPS * tile + TAPS)
            return (S[:, k % S_BUFS, of_s, :].rearrange("p s (r c) -> p s r c", c=W),
                    hy[:, s, :].unsqueeze(3).to_broadcast([128, TAPS, ROWS, W]),
                    hx[:, s, :].unsqueeze(2).to_broadcast([128, TAPS, ROWS, W]))

        def image(k):
            return gpad[:, k % 2, 2:2 + H, 1:1 + W]

        block = ctx.enter_context(nc.Block())

        @block.sync
        def _(sp):
            pair = lambda a, k: a[2 * k:2 * k + 2].rearrange("b c h w -> (b c) (h w)")
            sp.dma_start(x_sb[:, 0, :], pair(x, 0)).then_inc(x_in[0], 16)
            sp.dma_start(woff_nat[:], w_off.rearrange("o c a b -> o (c a b)").unsqueeze(1).to_broadcast([27, 2, C * TAPS])).then_inc(woff_in, 16)
            sp.wait_ge(zeroed, 1)
            for g in range(4):
                sp.dma_start(boff_col[OFFC * g:OFFC * g + 27, :], b_off.rearrange("(a b) -> a b", b=1)).then_inc(bias_in, 16)
            for k in range(1, PAIRS):
                sp.dma_start(x_sb[:, k, :], pair(x, k)).then_inc(x_in[k], 16)
            first = (LOW - 1) * C
            sp.dma_start(wconv_nat[:, :, 1, :], w_conv[:, first:].rearrange("o (t c) -> o t c", c=C)).then_inc(wrest_in, 16)
            sp.dma_start(w1_nat[:], w1.unsqueeze(1).to_broadcast([C, 2, C])).then_inc(wrest_in, 16)
            for h in range(2):
                sp.dma_start(b1_col[C * h:C * h + C, :], b1.rearrange("(a b) -> a b", b=1)).then_inc(b1_in, 16)
            for k in range(PAIRS):
                sp.wait_ge(y_ready, k + 1)
                sp.dma_start(pair(out, k), y_sb[:, k, :]).then_inc(stored, 16)
            sp.wait_ge(stored, 16 * PAIRS)

        @block.gpsimd
        def _(pool):
            nc.gpsimd.memset(boff_col[:], 0.0).then_inc(zeroed, 1)
            nc.gpsimd.memset(warm[:], 0.0).then_inc(zeroed, 1)
            nc.gpsimd.memset(woff_T[:], 0.0).then_inc(zeroed, 1)
            nc.gpsimd.memset(gpad[:], 0.0).then_inc(zeroed, 1)
            nc.gpsimd.memset(grows[:], 0.0).then_inc(zeroed, 1)
            nc.gpsimd.memset(wconv_T[:, 0, :], 0.0).then_inc(zeroed, 1)
            nc.gpsimd.memset(w1_T[:], 0.0).then_inc(zeroed, 1)

            def power(part):
                i, n, lo, hi = part
                pool.wait_ge(gn_var[i], n + 1)
                if part == GN1_FIRST:
                    pool.wait_ge(table_in, 16)
                nc.gpsimd.tensor_tensor(rstd[:, i, lo:hi], var[:, i, lo:hi], minus_half[:, lo:hi], ALU.pow).then_inc(gn_rstd[i], 1)

            def multiply(k, tile):
                pool.wait_ge(hy_masked, hats_count(k, tile // 2))
                if k >= S_BUFS:
                    pool.wait_ge(ring_full, index["turn", k - S_BUFS, last_group(tile)] + 1)
                o, a, b = S_part(k, tile)
                nc.gpsimd.tensor_tensor(o, a, b, ALU.mult).then_inc(S_pool, 1)

            def mask_rows(k):
                for js in halves(k):
                    pool.wait_ge(hats_ready, hats_count(k, js[-1]))
                    hy = hats[:, k % 2, js[0]:js[-1] + 1, 0:2 * TAPS * ROWS].rearrange("p j (s r) -> p j s r", r=ROWS)
                    m = mask[:, k % 2, 2 * js[0]:2 * js[-1] + 2].rearrange("p (j t) s -> p j (t s)", t=2)
                    nc.gpsimd.tensor_tensor(hy, hy, m.unsqueeze(3).to_broadcast([128, len(js), 2 * TAPS, ROWS]),
                                            ALU.mult).then_inc(hy_masked, 1)

            def square(k):
                for b in range(2):
                    wait_emptied(pool, index["sim", k, b])
                    if k >= 1:
                        pool.wait_ge(att_done, k)
                    nc.gpsimd.tensor_tensor(sim2[:, b], sim[:, b], sim[:, b], ALU.mult).then_inc(sim2_ready, 1)

            power(GN1_FIRST)
            power(GN1_REST)
            mask_rows(0)
            multiply(0, POOL_TILE)
            for k in range(PAIRS + 1):
                if k >= 1:
                    power(gn2(k - 1))
                if k + 1 < PAIRS:
                    mask_rows(k + 1)
                if 1 <= k < PAIRS:
                    square(k - 1)
                if k + 1 < PAIRS:
                    multiply(k + 1, POOL_TILE)

        @block.tensor
        def _(pe):
            def warm_up(n, ps):
                for _ in range(n):
                    pe.matmul(ps, warm_w[:, 0:128], warm_w[:, 0:ps.shape[1]], start=True, stop=True)

            def turn_weights():
                pe.wait_ge(woff_in, 16)
                for t in range(TAPS):
                    warm_up(1, out_ps[:, 0:128])
                    mm = pe.transpose(att_ps[:, OFFC * t:OFFC * t + 27], woff_nat[:, :, t:C * TAPS:TAPS], ident[0:27, 0:27])
                mm.then_inc(w_turned, 1)

            def turn_more_weights():
                pe.wait_ge(wrest_in, 48)
                for t in range(LOW):
                    pe.transpose(samp_ps[:, 0, C * t:C * t + C], wconv_nat[:, t, :, :].rearrange("o h c -> o (h c)"), ident[0:C, 0:C])
                pe.transpose(samp_ps[:, 0, C * LOW:C * LOW + C], w1_nat[:].rearrange("o h c -> o (h c)"), ident[0:C, 0:C]).then_inc(w_turned, 1)

            def group_means(part):
                i, n, lo, hi = part
                pe.wait_ge(gn_mv[i], hi - lo if i == 0 and n == 0 else hi)
                if part == GN1_REST:
                    pe.wait_ge(woff_ready, 2)
                if part == gn2(0):
                    pe.wait_ge(gn_var[0], 2)
                if i == 1 and n >= 1:
                    pe.wait_ge(y_own, n)
                pe.matmul(group_ps(part), average, mv[:, i, lo:hi, :], start=True, stop=True).then_inc(gn_group[i], 1)

            def convolve(k):
                pe.wait_ge(g_ready[0], k + 1)
                if k == 0:
                    pe.wait_ge(woff_ready, 2)
                if k >= 1:
                    pe.wait_ge(xT_out, k)
                for t in range(TAPS):
                    for j in range(2):
                        r, c = 8 * j + 1 + t // 3, t % 3
                        mm = pe.matmul(prep_ps[64 * j:64 * j + 64, 0:HALF], woff_T[:, t, :],
                                       gpad[:, k % 2, r:r + 8, c:c + W], start=(t == 0), stop=(t == TAPS - 1))
                mm.then_inc(conv_done, 1)

            def turn_offsets(k):
                pe.wait_ge(conv_out, k + 1)
                pe.transpose(prep_ps[:, 128:256], conv_sb[:], ident).then_inc(off_turned, 1)

            def turn_image(k):
                pe.wait_ge(dist_ready, 4 * (k + 1))
                if not general:
                    pe.wait_ge(reach_own, k + 1)
                pe.wait_ge(rows_ready, k + 1)
                for w, r in enumerate(BLOCK_ROWS):
                    mm = pe.transpose(prep_ps[:, 128 * w:128 * w + 128],
                                      grows[:, k % 2, r:r + 8, :].rearrange("p r c -> p (r c)"), ident)
                mm.then_inc(xT_done, 1)

            def turn(k, tile):
                for g in range(GROUPS):
                    if tile_of_group(g) != tile:
                        continue
                    i = index["turn", k, g]
                    pe.wait_ge(S_pool if tile == POOL_TILE else S_dve, S_count(k, tile, tile == POOL_TILE))
                    if i >= RING:
                        wait_emptied(pe, i - RING)
                    for n in range(GROUP):
                        s, w = divmod(GROUP * g + n, BLOCKS)
                        mm = pe.transpose(ring[i % RING][:, 128 * n:128 * n + 128],
                                          S[:, k % S_BUFS, s, 128 * w:128 * w + 128], ident)
                    mm.then_inc(ring_full, 1)

            def sample(k, tile):
                j, b = divmod(tile, 2)
                wait_emptied_up_to(pe, index["turn", k, last_group(tile)])
                pe.wait_ge(xT_out, k + 1)
                if k == 0 and tile == 0:
                    pe.wait_ge(wrest_ready, 1)
                if TILES * k + tile >= 1:
                    pe.wait_ge(samp_out, TILES * k + tile)
                for a in range(2):
                    for w in range(BLOCKS):
                        for h in range(2):
                            s = TAPS * tile + (LOW - 1) * h
                            mm = pe.matmul(samp_ps[64 * h:64 * h + 64, a, 0:LOW * 64], xT[:, k % 2, w if general else 2 * j + a, C * b:C * b + C],
                                           ST[:, k % 2, s:s + LOW, w, 64 * a:64 * a + 64],
                                           start=(w == 0), stop=(w == BLOCKS - 1))
                mm.then_inc(samp_done, 1)

            def project(k):
                pe.wait_ge(samp_out, TILES * (k + 1))
                if k >= 1:
                    pe.wait_ge(x1_ready, k)
                for t in range(LOW):
                    for b in range(2):
                        mm = pe.matmul(out_ps[64 * b:64 * b + 64, 0:N], wconv_T[:, t, :], sampled[:, k % 2, b, t, :],
                                       start=(t == 0), stop=(t == LOW - 1))
                mm.then_inc(out_done, 1)

            def norms_and_t(k):
                pe.wait_ge(g_ready[1], k + 1)
                pe.matmul(att_ps[:, N:2 * N], w1_T[:], g2[:, k % 2, :], start=True, stop=True)
                pe.wait_ge(sq_ready, k + 1)
                if k == 0:
                    pe.wait_ge(table_rest_in, 16)
                pe.matmul(att_ps[:, 0:N], ones_block, g2_sq[:], start=True, stop=True).then_inc(norm_t_done, 1)

            def turn_t(k):
                pe.wait_ge(t_ready, k + 1)
                for m in range(2):
                    mm = pe.transpose(att_ps[:, 128 * m:128 * m + 128], t_scaled[:, 128 * m:128 * m + 128], ident)
                mm.then_inc(tT_done, 1)

            def similarities(k):
                for b in range(2):
                    i = index["sim", k, b]
                    wait_emptied(pe, i - RING)
                    for m in range(2):
                        g = g2[64 * b:64 * b + 64, k % 2, :]
                        mm = pe.matmul(ring[i % RING][:, N * m:N * m + N], g[:, 128 * m:128 * m + 128], g,
                                       start=True, stop=True)
                    mm.then_inc(ring_full, 1)

            def attend(k):
                pe.wait_ge(tT_out, k + 1)
                if k < PAIRS - 1:
                    pe.wait_ge(sim2_ready, 2 * k + 2)
                else:
                    pe.wait_ge(sim2_last, 2)
                for m in range(2):
                    for b in range(2):
                        mm = pe.matmul(att_ps[64 * b:64 * b + 64, N:2 * N], tT[:, m, 64 * b:64 * b + 64],
                                       sim2[:, b, m, :], start=(m == 0), stop=(m == 1))
                mm.then_inc(att_done, 1)

            def turn_reach():
                pe.wait_ge(reach_ready, 1)
                pe.wait_ge(xT_out, PAIRS)
                pe.transpose(prep_ps[0:1, 0:128], reach[:, PAIRS:PAIRS + 1], ident).then_inc(reach_turned, 1)

            pe.wait_ge(warm_zeroed, 1)
            warm_up(14, out_ps[:, 0:N])
            pe.wait_ge(table_in, 16)
            group_means(GN1_FIRST)
            turn_weights()
            warm_up(6, out_ps[:, 0:N])
            convolve(0)
            group_means(GN1_REST)
            turn_offsets(0)
            turn_more_weights()
            warm_up(6, out_ps[:, 0:N])
            turn_image(0)
            warm_up(4, out_ps[:, 0:N])
            turn(0, 0)
            for k in range(PAIRS + 1):
                main, after = k < PAIRS, k >= 1
                ahead = k + 1 < PAIRS
                if ahead and k >= 1:
                    convolve(k + 1)
                if main:
                    turn(k, 1)
                if ahead and k == 0:
                    convolve(k + 1)
                if k == PAIRS:
                    warm_up(12, samp_ps[:, 0, 0:N])
                if after:
                    group_means(gn2(k - 1))
                if main:
                    sample(k, 0)
                if k == PAIRS:
                    warm_up(20, samp_ps[:, 0, 0:N])
                if main:
                    turn(k, 2)
                if ahead:
                    turn_offsets(k + 1)
                if main:
                    sample(k, 1)
                    turn(k, 3)
                if after:
                    norms_and_t(k - 1)
                if main:
                    sample(k, 2)
                if ahead:
                    turn_image(k + 1)
                if k == PAIRS - 1 and not general:
                    turn_reach()
                if after:
                    similarities(k - 1)
                    turn_t(k - 1)
                if main:
                    sample(k, 3)
                if ahead:
                    turn(k + 1, 0)
                if after:
                    attend(k - 1)
                if main:
                    project(k)

        @block.scalar
        def _(act):
            act.dma_start(table[:, 0:early], consts[:, 0:early]).then_inc(table_in, 16)
            act.dma_start(table[:, early:], consts[:, early:]).then_inc(table_rest_in, 16)
            act.wait_ge(zeroed, 2)
            nc.scalar.activation(warm[:], warm[:], ACT.Sigmoid)
            act.dma_start(wconv_nat[:, :, 0, :], w_conv[:, 0:LOW * C].rearrange("o (t c) -> o t c", c=C)).then_inc(wrest_in, 16)
            act.wait_ge(w_turned, 1)
            act.wait_ge(zeroed, 3)
            turned = att_ps[64:128, 0:TAPS * OFFC].rearrange("p (t o) -> p t o", o=OFFC)[:, :, 0:27]
            nc.scalar.copy(woff_T[64:128, :, OFFC:OFFC + 27], turned).then_inc(woff_ready, 1)

            def normalised_rows(k):
                act.wait_ge(gn_shift[0], 1 if k == 0 else 2)
                if k == 0:
                    act.wait_ge(zeroed, 5)
                if k >= 2:
                    act.wait_ge(xT_done, k - 1)
                nc.scalar.activation(grows[:, k % 2, 2:2 + H, :].rearrange("p r c -> p (r c)"), x_sb[:, k, :], ACT.Identity,
                                     bias=shift[:, 0, k:k + 1], scale=rstd[:, 0, k:k + 1]).then_inc(rows_ready, 1)

            def conv_bias(k):
                act.wait_ge(conv_done, k + 1)
                if k == 0:
                    act.wait_ge(bias_in, 64)
                if k >= 1:
                    act.wait_ge(off_turned, k)
                nc.scalar.activation(conv_sb[:], prep_ps[:, 0:HALF], ACT.Identity, bias=boff_col[:, 0:1]).then_inc(conv_out, 1)

            def weights_out():
                act.wait_ge(w_turned, 2)
                act.wait_ge(zeroed, 7)
                nc.scalar.copy(wconv_T[:, 1:LOW, :], samp_ps[:, 0, C:C * LOW].rearrange("p (t o) -> p t o", o=C))
                nc.scalar.copy(wconv_T[0:64, 0, :], samp_ps[0:64, 0, 0:C])
                nc.scalar.copy(w1_T[0:64, 0:64], samp_ps[0:64, 0, C * LOW:C * LOW + C])
                nc.scalar.copy(w1_T[64:128, 64:128], samp_ps[64:128, 0, C * LOW:C * LOW + C]).then_inc(wrest_ready, 1)

            def make_mask(k):
                act.wait_ge(off_turned, k + 1)
                offs = prep_ps[:, 128:256].rearrange("p (t o) -> p t o", o=OFFC)
                nc.scalar.activation(mask[:, k % 2], offs[:, :, 2 * TAPS:3 * TAPS], ACT.Sigmoid).then_inc(mask_ready, 1)

            def image_out(k):
                act.wait_ge(xT_done, k + 1)
                if k >= 2:
                    act.wait_ge(samp_done, TILES * (k - 1))
                n = len(BLOCK_ROWS) * 128
                nc.scalar.copy(xT[:, k % 2].rearrange("p w c -> p (w c)"), prep_ps[:, 0:n]).then_inc(xT_out, 1)

            def groups_out(k, tile):
                for g in range(GROUPS):
                    if tile_of_group(g) != tile or g in DVE_GROUPS:
                        continue
                    i = index["turn", k, g]
                    act.wait_ge(ring_full, i + 1)
                    if k >= 2:
                        act.wait_ge(samp_done, TILES * (k - 1))
                    dst = ST[:, k % 2].rearrange("p s w q -> p (s w q)")[:, 512 * g:512 * g + 512]
                    nc.scalar.copy(dst, ring[i % RING][:]).then_inc(ring_act, 1)

            def sampled_out(k, tile):
                j, b = divmod(tile, 2)
                act.wait_ge(samp_done, TILES * k + tile + 1)
                if k >= 2:
                    act.wait_ge(out_done, k - 1)
                dst = sampled[:, k % 2, b, :, HALF * j:HALF * j + HALF].rearrange("p t (a q) -> p a t q", a=2)
                src = samp_ps[:, :, 0:LOW * 64].rearrange("p a (t q) -> p a t q", t=LOW)
                nc.scalar.copy(dst, src).then_inc(samp_out, 1)

            def squares(k):
                act.wait_ge(g_ready[1], k + 1)
                if k >= 1:
                    act.wait_ge(norm_t_done, k)
                nc.scalar.activation(g2_sq[:], g2[:, k % 2, :], ACT.Square).then_inc(sq_ready, 1)

            def t_out(k):
                act.wait_ge(tT_done, k + 1)
                if k >= 1:
                    act.wait_ge(att_done, k)
                nc.scalar.copy(tT[:].rearrange("p m c -> p (m c)"), att_ps[:, 0:N]).then_inc(tT_out, 1)

            def relu_similarities(k):
                for b in range(2):
                    i = index["sim", k, b]
                    act.wait_ge(ring_full, i + 1)
                    if k >= 1:
                        act.wait_ge(sim2_ready, 2 * k)
                    nc.scalar.activation(sim[:, b].rearrange("p m n -> p (m n)"), ring[i % RING][:], ACT.Relu).then_inc(ring_act, 1)

            normalised_rows(0)
            conv_bias(0)
            make_mask(0)
            weights_out()
            image_out(0)
            groups_out(0, 0)
            normalised_rows(1)
            for k in range(PAIRS + 1):
                main, after = k < PAIRS, k >= 1
                ahead = k + 1 < PAIRS
                if ahead and k >= 1:
                    conv_bias(k + 1)
                if main:
                    groups_out(k, 1)
                if ahead and k == 0:
                    conv_bias(k + 1)
                if main:
                    sampled_out(k, 0)
                    groups_out(k, 2)
                if ahead:
                    make_mask(k + 1)
                if after:
                    squares(k - 1)
                if main:
                    sampled_out(k, 1)
                if main:
                    groups_out(k, 3)
                    sampled_out(k, 2)
                if ahead:
                    image_out(k + 1)
                if after:
                    relu_similarities(k - 1)
                    t_out(k - 1)
                if k + 2 < PAIRS:
                    normalised_rows(k + 2)
                if main:
                    sampled_out(k, 3)
                if ahead:
                    groups_out(k + 1, 0)

        @block.vector
        def _(dve):
            nc.vector.memset(warm_w[:], 0.0).then_inc(warm_zeroed, 1)
            own = [0, 0]

            def statistics(i, k):
                if i == 0:
                    dve.wait_ge(x_in[k], 16)
                else:
                    dve.wait_ge(x1_ready, k + 1)
                src = (x_sb if i == 0 else x1_sb)[:, k, :]
                nc.vector.bn_stats(stats6[:, i, k, :], src).then_inc(gn_own[i], 1)
                own[i] += 1
                dve.wait_ge(gn_own[i], own[i])
                nc.vector.bn_aggr(mv[:, i, k, :], stats6[:, i, k, :]).then_inc(gn_mv[i], 1)

            def group_variance(part):
                i, n, lo, hi = part
                dve.wait_ge(gn_group[i], n + 1)
                nc.vector.tensor_copy(gmv[:, i, lo:hi, :], group_ps(part)).then_inc(gn_own[i], 1)
                nc.vector.tensor_tensor(gdiff[:, i, lo:hi], group_ps(part)[:, :, 0], mv[:, i, lo:hi, 0],
                                        ALU.subtract).then_inc(gn_own[i], 1)
                dve.wait_ge(gn_own[i], own[i] + 2)
                nc.vector.tensor_tensor(var[:, i, lo:hi], gdiff[:, i, lo:hi], gdiff[:, i, lo:hi], ALU.mult).then_inc(gn_own[i], 1)
                own[i] += 3
                dve.wait_ge(gn_own[i], own[i])
                nc.vector.scalar_tensor_tensor(out=var[:, i, lo:hi], in0=gmv[:, i, lo:hi, 1], scalar=EPS_GN,
                                               in1=var[:, i, lo:hi], op0=ALU.add, op1=ALU.add).then_inc(gn_var[i], 1)

            def scale_and_shift(part):
                i, n, lo, hi = part
                dve.wait_ge(gn_rstd[i], n + 1)
                nc.vector.scalar_tensor_tensor(out=shift[:, i, lo:hi], in0=gmv[:, i, lo:hi, 0], scalar=-1.0,
                                               in1=rstd[:, i, lo:hi], op0=ALU.mult, op1=ALU.mult).then_inc(gn_shift[i], 1)
                dve.wait_ge(gn_shift[i], n + 1)

            def normalise(i, k):
                if i == 0:
                    src, dst = x_sb[:, k, :].rearrange("p (h w) -> p h w", w=W), image(k)
                    if k == 0:
                        dve.wait_ge(zeroed, 4)
                    if k >= 2:
                        dve.wait_ge(xT_done, k - 1)
                else:
                    src, dst = x1_sb[:, k, :], g2[:, k % 2, :]
                nc.vector.tensor_scalar(dst, src, rstd[:, i, k:k + 1], shift[:, i, k:k + 1], ALU.mult, ALU.add).then_inc(g_ready[i], 1)

            def distances(k, j):
                if j == 0:
                    dve.wait_ge(mask_ready, k + 1)
                if k == 0 and j == 0:
                    dve.wait_ge(table_rest_in, 16)
                if k >= 2:
                    dve.wait_ge(S_pool, S_count(k - 2, TILES - 1, True))
                    dve.wait_ge(S_dve, S_count(k - 2, TILES - 1, False))
                offs = prep_ps[:, 128:256].rearrange("p (t o) -> p t o", o=OFFC)
                ty, tx = (h.rearrange("p (t s) r -> p t s r", s=TAPS) for h in hats_of(k, j))
                rows = cy[:, j, :] if general else cy_window
                for n, (t, of, size) in enumerate(((ty, rows, ROWS), (tx, cx, W))):
                    nc.vector.tensor_tensor(t, offs[:, 2 * j:2 * j + 2, TAPS * n:TAPS * n + TAPS].unsqueeze(3).to_broadcast([128, 2, TAPS, size]),
                                            of.unsqueeze(1).unsqueeze(1).to_broadcast([128, 2, TAPS, size]),
                                            ALU.add).then_inc(dist_ready, 1)
                if j == 1 and not general:
                    nc.vector.tensor_reduce(reach[:, k:k + 1], offs[:, :, 0:TAPS], AX.XY, ALU.max,
                                            apply_absolute_value=True).then_inc(reach_own, 1)

            def make_hats(k, js):
                dve.wait_ge(dist_ready, 4 * k + 2 * js[-1] + 2)
                h = hats[:, k % 2, js[0]:js[-1] + 1, :]
                bits = h.bitcast(mybir.dt.int32)
                nc.vector.tensor_scalar(bits, bits, 0x7FFFFFFF, None, ALU.bitwise_and).then_inc(abs_ready, 1)
                dve.wait_ge(abs_ready, hats_count(k, js[-1]))
                nc.vector.tensor_scalar(h, h, 1.0, -1.0, ALU.min, ALU.add).then_inc(hats_ready, 1)

            def farthest():
                dve.wait_ge(reach_own, PAIRS)
                nc.vector.tensor_reduce(reach[:, PAIRS:PAIRS + 1], reach[:, 0:PAIRS], AX.X, ALU.max).then_inc(reach_ready, 1)

            def set_far():
                dve.wait_ge(reach_turned, 1)
                nc.vector.tensor_reduce(reach[0:1, PAIRS + 1:PAIRS + 2], prep_ps[0:1, 0:128], AX.X, ALU.max).then_inc(reach_own, 1)
                dve.wait_ge(reach_own, PAIRS + 1)
                nc.vector.tensor_scalar(far, reach[0:1, PAIRS + 1:PAIRS + 2], float(REACH), None, ALU.is_gt).then_inc(far_set, 1)

            def multiply(k, tile):
                dve.wait_ge(hy_masked, hats_count(k, tile // 2))
                if k >= S_BUFS:
                    dve.wait_ge(ring_full, index["turn", k - S_BUFS, last_group(tile)] + 1)
                o, a, b = S_part(k, tile)
                nc.vector.tensor_tensor(o, a, b, ALU.mult).then_inc(S_dve, 1)

            def groups_out(k, tile):
                for g in range(GROUPS):
                    if tile_of_group(g) != tile or g not in DVE_GROUPS:
                        continue
                    i = index["turn", k, g]
                    dve.wait_ge(ring_full, i + 1)
                    if k >= 2:
                        dve.wait_ge(samp_done, TILES * (k - 1))
                    dst = ST[:, k % 2].rearrange("p s w q -> p (s w q)")[:, 512 * g:512 * g + 512]
                    nc.vector.tensor_copy(dst, ring[i % RING][:]).then_inc(ring_dve, 1)

            def residual(k):
                dve.wait_ge(out_done, k + 1)
                nc.vector.tensor_tensor(x1_sb[:, k, :], out_ps[:, 0:N], x_sb[:, k, :], ALU.add).then_inc(x1_ready, 1)

            def square_last():
                for b in range(2):
                    wait_emptied(dve, index["sim", PAIRS - 1, b])
                    nc.vector.tensor_tensor(sim2[:, b], sim[:, b], sim[:, b], ALU.mult).then_inc(sim2_last, 1)

            def scale_t(k):
                dve.wait_ge(norm_t_done, k + 1)
                if k >= 1:
                    dve.wait_ge(y_own, k)
                nc.vector.tensor_scalar(norm2[:], att_ps[:, 0:N], EPS_NORM2, None, ALU.max).then_inc(norm2_ready, 1)
                dve.wait_ge(norm2_ready, k + 1)
                nc.vector.reciprocal(inv_norm2[:], norm2[:]).then_inc(inv_ready, 1)
                dve.wait_ge(inv_ready, k + 1)
                if k == 0:
                    dve.wait_ge(b1_in, 32)
                if k >= 1:
                    dve.wait_ge(tT_done, k)
                nc.vector.scalar_tensor_tensor(out=t_scaled[:], in0=att_ps[:, N:2 * N], scalar=b1_col[:, 0:1],
                                               in1=inv_norm2[:], op0=ALU.add, op1=ALU.mult).then_inc(t_ready, 1)

            def finish(k):
                dve.wait_ge(att_done, k + 1)
                y = y_sb[:, k, :]
                nc.vector.tensor_tensor(y, att_ps[:, N:2 * N], inv_norm2[:], ALU.mult).then_inc(y_own, 1)
                dve.wait_ge(y_own, k + 1)
                nc.vector.tensor_tensor(y, y, x1_sb[:, k, :], ALU.add).then_inc(y_ready, 1)

            statistics(0, 0)
            group_variance(GN1_FIRST)
            scale_and_shift(GN1_FIRST)
            normalise(0, 0)
            dve.wait_ge(w_turned, 1)
            dve.wait_ge(zeroed, 7)
            turned = att_ps[0:64, 0:TAPS * OFFC].rearrange("p (t o) -> p t o", o=OFFC)[:, :, 0:27]
            nc.vector.tensor_copy(woff_T[0:64, :, 0:27], turned).then_inc(woff_ready, 1)
            for k in range(1, PAIRS):
                statistics(0, k)
            group_variance(GN1_REST)
            distances(0, 0)
            make_hats(0, (0,))
            distances(0, 1)
            multiply(0, 0)
            make_hats(0, (1,))
            multiply(0, 1)
            scale_and_shift(GN1_REST)
            normalise(0, 1)
            groups_out(0, 0)
            for k in range(PAIRS + 1):
                main, after = k < PAIRS, k >= 1
                ahead = k + 1 < PAIRS
                if k == PAIRS - 1 and not general:
                    farthest()
                if after:
                    statistics(1, k - 1)
                if main:
                    groups_out(k, 1)
                    multiply(k, 3)
                if after:
                    group_variance(gn2(k - 1))
                    scale_and_shift(gn2(k - 1))
                    normalise(1, k - 1)
                if main:
                    groups_out(k, 2)
                if ahead:
                    distances(k + 1, 0)
                    distances(k + 1, 1)
                    make_hats(k + 1, (0, 1))
                if main:
                    groups_out(k, 3)
                if after:
                    scale_t(k - 1)
                if ahead:
                    multiply(k + 1, 0)
                if k + 2 < PAIRS:
                    normalise(0, k + 2)
                if k == PAIRS - 1 and not general:
                    set_far()
                if k == PAIRS:
                    square_last()
                if after:
                    finish(k - 1)
                if ahead:
                    groups_out(k + 1, 0)
                    multiply(k + 1, 1)
                if main:
                    residual(k)
            if not general:
                dve.wait_ge(far_set, 1)


def build(nc, *args):
    with nc.sbuf_tensor("far", [1, 1], mybir.dt.int32) as far:
        run_pairs(nc, False, far[:], *args)
        too_far = nc.values_load(far[:], min_val=0, max_val=1)
        with nc.If(too_far > 0):
            run_pairs(nc, True, None, *args)


def kernel(x, L0_conv_w_off, L0_conv_b_off, L0_conv_w_conv, L1_conv_W, L1_conv_b):
    import concourse.bacc as bacc
    from concourse.bass_utils import run_bass_kernel_spmd

    nc = bacc.Bacc("TRN2", target_bir_lowering=False, num_devices=1)
    given = {"x": x, "w_off": L0_conv_w_off, "b_off": L0_conv_b_off, "w_conv": L0_conv_w_conv,
             "w1": L1_conv_W, "b1": L1_conv_b, "consts": constants()}
    arrays = {name: np.ascontiguousarray(a) for name, a in given.items()}
    args = [nc.dram_tensor(name, a.shape, mybir.dt.from_np(a.dtype), kind="ExternalInput").ap()
            for name, a in arrays.items()]
    out = nc.dram_tensor("out", (B, C, H, W), F32, kind="ExternalOutput").ap()
    build(nc, *args, out)
    result = run_bass_kernel_spmd(nc, [arrays], core_ids=[0])
    return result.results[0]["out"]
```

```python
from contextlib import ExitStack

import numpy as np

import concourse.bass as bass
from concourse import mybir

F32 = mybir.dt.float32
ALU = mybir.AluOpType
ACT = mybir.ActivationFunctionType
AX = mybir.AxisListType

B, C, H, W = 8, 64, 16, 16
N = H * W
TAPS = 9
PAIRS = B // 2
HALF = N // 2
TILES = 4
LOW = 5
PADR, PADC = H + 4, W + 2
GROUP = 4
RING = 3
REACH = 2
EPS_GN = 1e-5
EPS_NORM2 = 1e-8 ** 2
OFFC = 32


def constants():
    p = np.arange(128)
    ident = np.eye(128)
    average = (p[:, None] // 2 == p[None, :] // 2) * 0.5
    ones = (p[:, None] // C == p[None, :] // C) * 1.0
    row = p[:, None] // W
    cy = np.concatenate([8 * j + row - np.arange(H) for j in range(2)], 1)
    cy_window = row % 4 + REACH - np.arange(8)
    cx = (p[:, None] % W) - np.arange(W)
    power = np.full((128, PAIRS), -0.5)
    return np.concatenate([ident, average, power, ones, cy, cy_window, cx], 1).astype(np.float32)


def run_pairs(nc, general, far, y_sb, stored, x, w_off, b_off, w_conv, w1, b1, consts, out):
    BLOCKS = 2 if general else 1
    ROWS = 8 * BLOCKS
    BLOCK_ROWS = [2, 10] if general else [0, 4, 8, 12]
    SLOTS = TILES * TAPS * BLOCKS
    GROUPS = SLOTS // GROUP
    S_BUFS = 1 if general else 2
    POOL_TILE = 1
    DVE_GROUPS = (1, 4, 7, 10, 13, 16) if general else (6,)

    way = "general_" if general else ""
    ctx = ExitStack()
    with ctx:
        def sb(name, shape):
            return ctx.enter_context(nc.sbuf_tensor(way + name, shape, F32))

        def sem(name):
            return ctx.enter_context(nc.semaphore(way + name))

        x_sb = sb("x_sb", [128, PAIRS, N])
        x1_sb = sb("x1_sb", [128, PAIRS, N])
        table = sb("table", [128, consts.shape[1]])
        woff_nat = sb("woff_nat", [27, 2, C * TAPS])
        wconv_nat = sb("wconv_nat", [C, LOW, 2, C])
        w1_nat = sb("w1_nat", [C, 2, C])
        boff_col = sb("boff_col", [128, 1])
        b1_col = sb("b1_col", [128, 1])
        woff_T = sb("woff_T", [128, TAPS, 2 * OFFC])
        wconv_T = sb("wconv_T", [128, LOW, C])
        w1_T = sb("w1_T", [128, 128])
        gpad = sb("gpad", [128, 2, PADR, PADC])
        grows = sb("grows", [128, 2, PADR, W])
        conv_sb = sb("conv_sb", [128, 128])
        hats = sb("hats", [128, 2, 2, 2 * TAPS * (ROWS + W)])
        mask = sb("mask", [128, 2, TILES, TAPS])
        S = sb("S", [128, S_BUFS, TILES * TAPS, BLOCKS * 128])
        ST = sb("ST", [128, 2, TILES * TAPS, BLOCKS, 128])
        xT = sb("xT", [128, 2, len(BLOCK_ROWS), 128])
        sampled = sb("sampled", [128, 2, 2, LOW, N])
        g2 = sb("g2", [128, 2, N])
        g2_sq = sb("g2_sq", [128, N])
        inv_norm2 = sb("inv_norm2", [128, N])
        norm2 = sb("norm2", [128, N])
        inv_pixel = sb("inv_pixel", [128, 4])
        b1_rows = sb("b1_rows", [128, 2, C])
        t_scaled = sb("t_scaled", [128, N])
        tT = sb("tT", [128, 2, 128])
        sim = sb("sim", [128, 2, 2, N])
        sim2 = sb("sim2", [128, 2, 2, N])
        stats6 = sb("stats6", [128, 2, PAIRS, 6])
        mv = sb("mv", [128, 2, PAIRS, 2])
        gmv = sb("gmv", [128, 2, PAIRS, 2])
        gdiff = sb("gdiff", [128, 2, PAIRS])
        var = sb("var", [128, 2, PAIRS])
        rstd = sb("rstd", [128, 2, PAIRS])
        shift = sb("shift", [128, 2, PAIRS])
        warm = sb("warm", [128, 1])
        warm_w = ctx.enter_context(nc.sbuf_tensor(way + "warm_w", [128, N], mybir.dt.bfloat16))

        reach = sb("reach", [128, PAIRS + 2])
        ident = table[:, 0:128]
        average = table[:, 128:256]
        minus_half = table[:, 256:256 + PAIRS]
        early = 256 + PAIRS
        ones_block = table[:, early:early + 128]
        late = table[:, early + 128:]
        cy = late[:, 0:32].rearrange("p (j r) -> p j r", j=2)
        cy_window = late[:, 32:40]
        cx = late[:, 40:40 + W]

        ring = [ctx.enter_context(nc.psum_tensor(way + f"ring{i}", [128, 512], F32)) for i in range(RING)]
        samp_ps = ctx.enter_context(nc.psum_tensor(way + "samp_ps", [128, 2, 512], F32))
        out_ps = ctx.enter_context(nc.psum_tensor(way + "out_ps", [128, 512], F32))
        prep_ps = ctx.enter_context(nc.psum_tensor(way + "prep_ps", [128, 512], F32))
        att_ps = ctx.enter_context(nc.psum_tensor(way + "att_ps", [128, 512], F32))

        x_in = [sem(f"x_in{k}") for k in range(PAIRS)]
        table_in, table_rest_in, woff_in, wrest_in, bias_in, b1_in = sem("table_in"), sem("table_rest_in"), sem("woff_in"), sem("wrest_in"), sem("bias_in"), sem("b1_in")
        zeroed, warm_zeroed, samp_zeroed = sem("zeroed"), sem("warm_zeroed"), sem("samp_zeroed")
        w_turned, woff_ready, wrest_ready = sem("w_turned"), sem("woff_ready"), sem("wrest_ready")
        gn_own = [sem("gn1_own"), sem("gn2_own")]
        gn_mv = [sem("gn1_mv"), sem("gn2_mv")]
        gn_group = [sem("gn1_group"), sem("gn2_group")]
        gn_var = [sem("gn1_var"), sem("gn2_var")]
        gn_rstd = [sem("gn1_rstd"), sem("gn2_rstd")]
        gn_shift = [sem("gn1_shift"), sem("gn2_shift")]
        g_ready = [sem("g1_ready"), sem("g2_ready")]
        rows_ready, conv_done, conv_out, off_turned = sem("rows_ready"), sem("conv_done"), sem("conv_out"), sem("off_turned")
        dist_ready, mask_ready, abs_ready, hats_ready, hy_masked = (
            sem("dist_ready"), sem("mask_ready"), sem("abs_ready"), sem("hats_ready"), sem("hy_masked"))
        xT_done, xT_out = sem("xT_done"), sem("xT_out")
        S_dve, S_pool = sem("S_dve"), sem("S_pool")
        ring_full, ring_act, ring_dve = sem("ring_full"), sem("ring_act"), sem("ring_dve")
        samp_done, samp_out = sem("samp_done"), sem("samp_out")
        out_done, x1_ready = sem("out_done"), sem("x1_ready")
        sq_ready, norm_t_done, norm2_ready, inv_ready, t_ready = (
            sem("sq_ready"), sem("norm_t_done"), sem("norm2_ready"), sem("inv_ready"), sem("t_ready"))
        tT_done, tT_out = sem("tT_done"), sem("tT_out")
        sim2_ready, sim2_last, att_done, y_own, y_ready = (
            sem("sim2_ready"), sem("sim2_last"), sem("att_done"), sem("y_own"), sem("y_ready"))

        inv_spread, inv_kept, b1_rows_in = sem("inv_spread"), sem("inv_kept"), sem("b1_rows_in")
        reach_own, reach_ready, reach_turned, far_set = sem("reach_own"), sem("reach_ready"), sem("reach_turned"), sem("far_set")

        GN1_FIRST, GN1_REST = (0, 0, 0, 1), (0, 1, 1, PAIRS)

        def gn2(k):
            return (1, k, k, k + 1)

        def group_ps(part):
            n = part[3] - part[2]
            ps = prep_ps if part == GN1_FIRST else out_ps if part == gn2(PAIRS - 1) else att_ps
            return ps[:, 0:2 * n].rearrange("p (k s) -> p k s", s=2)

        items = []

        def tile_of_block(n):
            return n // (TAPS * BLOCKS)

        def tile_of_group(g):
            return tile_of_block(GROUP * g)

        def last_group(tile):
            return ((tile + 1) * TAPS * BLOCKS - 1) // GROUP

        for k in range(PAIRS + 1):
            for tile in range(TILES):
                if k < PAIRS:
                    items += [("turn", k, g) for g in range(GROUPS) if tile_of_group(g) == tile]
                if tile == 3 and k >= 1:
                    items += [("sim", k - 1, n) for n in range(4 if k == PAIRS else 2)]
        index = {item: i for i, item in enumerate(items)}
        by_dve = [item[0] == "turn" and item[2] in DVE_GROUPS for item in items]

        def emptied_by(engine_is_dve, i):
            return sum(1 for j in range(i + 1) if by_dve[j] == engine_is_dve)

        def wait_emptied(eng, i):
            eng.wait_ge(ring_dve if by_dve[i] else ring_act, emptied_by(by_dve[i], i))

        def wait_emptied_up_to(eng, i):
            for is_dve, s in ((False, ring_act), (True, ring_dve)):
                if emptied_by(is_dve, i):
                    eng.wait_ge(s, emptied_by(is_dve, i))

        def S_count(k, tile, on_pool):
            return sum(1 for n in range(TILES * k + tile + 1) if (n % TILES == POOL_TILE) == on_pool)

        def wait_S(eng, k, tile):
            on_pool = tile == POOL_TILE
            eng.wait_ge(S_pool if on_pool else S_dve, S_count(k, tile, on_pool))

        def hats_of(k, j):
            h = hats[:, k % 2, j, :]
            return (h[:, 0:2 * TAPS * ROWS].rearrange("p (s r) -> p s r", r=ROWS),
                    h[:, 2 * TAPS * ROWS:].rearrange("p (s c) -> p s c", c=W))

        def hats_count(k, j):
            return j + 1 if k == 0 else k + 2

        def S_part(k, tile):
            hy, hx = hats_of(k, tile // 2)
            s, of_s = slice(TAPS * (tile % 2), TAPS * (tile % 2) + TAPS), slice(TAPS * tile, TAPS * tile + TAPS)
            return (S[:, k % S_BUFS, of_s, :].rearrange("p s (r c) -> p s r c", c=W),
                    hy[:, s, :].unsqueeze(3).to_broadcast([128, TAPS, ROWS, W]),
                    hx[:, s, :].unsqueeze(2).to_broadcast([128, TAPS, ROWS, W]))

        def image(k):
            return gpad[:, k % 2, 2:2 + H, 1:1 + W]

        block = ctx.enter_context(nc.Block())

        @block.sync
        def _(sp):
            if general:
                sp.wait_ge(stored, 16 * PAIRS)
            pair = lambda a, k: a[2 * k:2 * k + 2].rearrange("b c h w -> (b c) (h w)")
            sp.dma_start(x_sb[:, 0, :], pair(x, 0)).then_inc(x_in[0], 16)
            sp.dma_start(woff_nat[:], w_off.rearrange("o c a b -> o (c a b)").unsqueeze(1).to_broadcast([27, 2, C * TAPS])).then_inc(woff_in, 16)
            sp.wait_ge(zeroed, 1)
            for g in range(4):
                sp.dma_start(boff_col[OFFC * g:OFFC * g + 27, :], b_off.rearrange("(a b) -> a b", b=1)).then_inc(bias_in, 16)
            for k in range(1, PAIRS):
                sp.dma_start(x_sb[:, k, :], pair(x, k)).then_inc(x_in[k], 16)
            first = (LOW - 1) * C
            sp.dma_start(wconv_nat[:, :, 1, :], w_conv[:, first:].rearrange("o (t c) -> o t c", c=C)).then_inc(wrest_in, 16)
            sp.dma_start(w1_nat[:], w1.unsqueeze(1).to_broadcast([C, 2, C])).then_inc(wrest_in, 16)
            for h in range(2):
                sp.dma_start(b1_col[C * h:C * h + C, :], b1.rearrange("(a b) -> a b", b=1)).then_inc(b1_in, 16)
            sp.dma_start(b1_rows[:], b1.unsqueeze(0).unsqueeze(0).to_broadcast([128, 2, C])).then_inc(b1_rows_in, 16)
            for k in range(PAIRS):
                sp.wait_ge(y_ready, k + 1)
                sp.dma_start(pair(out, k), y_sb[:, k, :]).then_inc(stored, 16)
            if general:
                sp.wait_ge(stored, 2 * 16 * PAIRS)

        @block.gpsimd
        def _(pool):
            nc.gpsimd.memset(boff_col[:], 0.0).then_inc(zeroed, 1)
            nc.gpsimd.memset(warm[:], 0.0).then_inc(zeroed, 1)
            nc.gpsimd.memset(woff_T[:], 0.0).then_inc(zeroed, 1)
            nc.gpsimd.memset(gpad[:], 0.0).then_inc(zeroed, 1)
            nc.gpsimd.memset(grows[:], 0.0).then_inc(zeroed, 1)
            nc.gpsimd.memset(w1_T[:], 0.0).then_inc(zeroed, 1)

            def power(part):
                i, n, lo, hi = part
                pool.wait_ge(gn_var[i], n + 1)
                if part == GN1_FIRST:
                    pool.wait_ge(table_in, 16)
                nc.gpsimd.tensor_tensor(rstd[:, i, lo:hi], var[:, i, lo:hi], minus_half[:, lo:hi], ALU.pow).then_inc(gn_rstd[i], 1)

            def multiply(k, tile):
                pool.wait_ge(hy_masked, hats_count(k, tile // 2))
                if k >= S_BUFS:
                    pool.wait_ge(ring_full, index["turn", k - S_BUFS, last_group(tile)] + 1)
                o, a, b = S_part(k, tile)
                nc.gpsimd.tensor_tensor(o, a, b, ALU.mult).then_inc(S_pool, 1)

            def mask_rows(k, js):
                pool.wait_ge(hats_ready, hats_count(k, js[-1]))
                hy = hats[:, k % 2, js[0]:js[-1] + 1, 0:2 * TAPS * ROWS].rearrange("p j (s r) -> p j s r", r=ROWS)
                m = mask[:, k % 2, 2 * js[0]:2 * js[-1] + 2].rearrange("p (j t) s -> p j (t s)", t=2)
                nc.gpsimd.tensor_tensor(hy, hy, m.unsqueeze(3).to_broadcast([128, len(js), 2 * TAPS, ROWS]),
                                        ALU.mult).then_inc(hy_masked, 1)

            def square(k):
                for b in range(2):
                    wait_emptied(pool, index["sim", k, b])
                    if k >= 1:
                        pool.wait_ge(att_done, k)
                    nc.gpsimd.tensor_tensor(sim2[:, b], sim[:, b], sim[:, b], ALU.mult).then_inc(sim2_ready, 1)

            power(GN1_FIRST)
            power(GN1_REST)
            mask_rows(0, (0,))
            multiply(0, POOL_TILE)
            mask_rows(0, (1,))
            for k in range(PAIRS + 1):
                if k >= 1:
                    power(gn2(k - 1))
                if k + 1 < PAIRS:
                    mask_rows(k + 1, (0, 1))
                    multiply(k + 1, POOL_TILE)
                if 1 <= k < PAIRS:
                    square(k - 1)

        @block.tensor
        def _(pe):
            def warm_up(n, ps):
                for _ in range(n):
                    pe.matmul(ps, warm_w[:, 0:128], warm_w[:, 0:ps.shape[1]], start=True, stop=True)

            def turn_weights():
                pe.wait_ge(woff_in, 16)
                for t in range(TAPS):
                    warm_up(1, out_ps[:, 0:128])
                    mm = pe.transpose(att_ps[:, OFFC * t:OFFC * t + 27], woff_nat[:, :, t:C * TAPS:TAPS], ident[0:27, 0:27])
                mm.then_inc(w_turned, 1)

            def turn_more_weights():
                pe.wait_ge(wrest_in, 48)
                for t in range(LOW):
                    pe.transpose(ring[RING - 1][:, C * t:C * t + C], wconv_nat[:, t, :, :].rearrange("o h c -> o (h c)"), ident[0:C, 0:C])
                pe.transpose(ring[RING - 1][:, C * LOW:C * LOW + C], w1_nat[:].rearrange("o h c -> o (h c)"), ident[0:C, 0:C]).then_inc(w_turned, 1)

            def group_means(part):
                i, n, lo, hi = part
                pe.wait_ge(gn_mv[i], hi - lo if i == 0 and n == 0 else hi)
                if part == GN1_REST:
                    pe.wait_ge(woff_ready, 2)
                if part == gn2(0):
                    pe.wait_ge(gn_var[0], 2)
                if i == 1 and 1 <= n < PAIRS - 1:
                    pe.wait_ge(y_own, n)
                if part == gn2(PAIRS - 1):
                    pe.wait_ge(x1_ready, PAIRS)
                pe.matmul(group_ps(part), average, mv[:, i, lo:hi, :], start=True, stop=True).then_inc(gn_group[i], 1)

            def convolve(k):
                pe.wait_ge(g_ready[0], k + 1)
                if k == 0:
                    pe.wait_ge(woff_ready, 2)
                if k >= 1:
                    pe.wait_ge(xT_out, k)
                for t in range(TAPS):
                    for j in range(2):
                        r, c = 8 * j + 1 + t // 3, t % 3
                        mm = pe.matmul(prep_ps[64 * j:64 * j + 64, 0:HALF], woff_T[:, t, :],
                                       gpad[:, k % 2, r:r + 8, c:c + W], start=(t == 0), stop=(t == TAPS - 1))
                mm.then_inc(conv_done, 1)

            def turn_offsets(k):
                pe.wait_ge(conv_out, k + 1)
                pe.transpose(prep_ps[:, 128:256], conv_sb[:], ident).then_inc(off_turned, 1)

            def turn_image(k):
                pe.wait_ge(dist_ready, 4 * (k + 1))
                if not general:
                    pe.wait_ge(reach_own, k + 1)
                pe.wait_ge(rows_ready, k + 1)
                for w, r in enumerate(BLOCK_ROWS):
                    mm = pe.transpose(prep_ps[:, 128 * w:128 * w + 128],
                                      grows[:, k % 2, r:r + 8, :].rearrange("p r c -> p (r c)"), ident)
                mm.then_inc(xT_done, 1)

            def turn(k, tile):
                for g in range(GROUPS):
                    if tile_of_group(g) != tile:
                        continue
                    i = index["turn", k, g]
                    for of in sorted({tile, tile_of_block(GROUP * g + GROUP - 1)}):
                        wait_S(pe, k, of)
                    if i == RING - 1:
                        pe.wait_ge(wrest_ready, 1)
                    if i >= RING:
                        wait_emptied(pe, i - RING)
                    for n in range(GROUP):
                        s, w = divmod(GROUP * g + n, BLOCKS)
                        mm = pe.transpose(ring[i % RING][:, 128 * n:128 * n + 128],
                                          S[:, k % S_BUFS, s, 128 * w:128 * w + 128], ident)
                    mm.then_inc(ring_full, 1)

            def sample(k, tile):
                j, b = divmod(tile, 2)
                wait_emptied_up_to(pe, index["turn", k, last_group(tile)])
                pe.wait_ge(xT_out, k + 1)
                if k == 0 and tile == 0:
                    pe.wait_ge(samp_zeroed, 2)
                if TILES * k + tile >= 1:
                    pe.wait_ge(samp_out, TILES * k + tile)
                for a in range(2):
                    for w in range(BLOCKS):
                        for h in range(2):
                            lo, hi = (0, LOW) if a == h else (0, LOW - 1) if h == 0 else (1, LOW)
                            s = TAPS * tile + (LOW - 1) * h
                            mm = pe.matmul(samp_ps[64 * h:64 * h + 64, a, 64 * lo:64 * hi], xT[:, k % 2, w if general else 2 * j + a, C * b:C * b + C],
                                           ST[:, k % 2, s + lo:s + hi, w, 64 * a:64 * a + 64],
                                           start=(w == 0), stop=(w == BLOCKS - 1))
                mm.then_inc(samp_done, 1)

            def project(k):
                pe.wait_ge(samp_out, TILES * (k + 1))
                if k >= 1:
                    pe.wait_ge(x1_ready, k)
                for t in range(LOW):
                    for b in range(2):
                        mm = pe.matmul(out_ps[64 * b:64 * b + 64, 0:N], wconv_T[:, t, :], sampled[:, k % 2, b, t, :],
                                       start=(t == 0), stop=(t == LOW - 1))
                mm.then_inc(out_done, 1)

            def norms_and_t(k):
                pe.wait_ge(g_ready[1], k + 1)
                pe.matmul(att_ps[:, N:2 * N], w1_T[:], g2[:, k % 2, :], start=True, stop=True)
                pe.wait_ge(sq_ready, k + 1)
                if k == 0:
                    pe.wait_ge(table_rest_in, 16)
                pe.matmul(att_ps[:, 0:N], ones_block, g2_sq[:], start=True, stop=True).then_inc(norm_t_done, 1)

            def norms_and_t_last():
                g, sq = g2[:, (PAIRS - 1) % 2, :], g2_sq[:]
                pe.wait_ge(g_ready[1], PAIRS)
                pe.wait_ge(y_own, PAIRS - 1)
                for m in range(2):
                    pe.matmul(att_ps[:, 128 * m:128 * m + 128], g[:, 128 * m:128 * m + 128], w1_T[:], start=True, stop=True)
                pe.wait_ge(sq_ready, PAIRS)
                for m in range(2):
                    mm = pe.matmul(att_ps[:, N + 128 * m:N + 128 * m + 128], sq[:, 128 * m:128 * m + 128], ones_block, start=True, stop=True)
                mm.then_inc(norm_t_done, 1)

            def spread_inverse():
                pe.wait_ge(inv_ready, PAIRS)
                pe.wait_ge(t_ready, PAIRS)
                for m in range(2):
                    for b in range(2):
                        mm = pe.matmul(att_ps[64 * b:64 * b + 64, 128 * m:128 * m + 128],
                                       inv_pixel[:, 2 * m + b:2 * m + b + 1].to_broadcast([128, 64]), ident, start=True, stop=True)
                mm.then_inc(inv_spread, 1)

            def turn_t(k):
                pe.wait_ge(t_ready, k + 1)
                for m in range(2):
                    mm = pe.transpose(att_ps[:, 128 * m:128 * m + 128], t_scaled[:, 128 * m:128 * m + 128], ident)
                mm.then_inc(tT_done, 1)

            def similarities(k):
                for b in range(2):
                    i = index["sim", k, b]
                    wait_emptied(pe, i - RING)
                    for m in range(2):
                        g = g2[64 * b:64 * b + 64, k % 2, :]
                        mm = pe.matmul(ring[i % RING][:, N * m:N * m + N], g[:, 128 * m:128 * m + 128], g,
                                       start=True, stop=True)
                    mm.then_inc(ring_full, 1)

            def similarities_last():
                for n in range(4):
                    b, m = divmod(n, 2)
                    i = index["sim", PAIRS - 1, n]
                    wait_emptied(pe, i - RING)
                    g = g2[64 * b:64 * b + 64, (PAIRS - 1) % 2, :]
                    pe.matmul(ring[i % RING][:, 0:N], g[:, 128 * m:128 * m + 128], g, start=True, stop=True).then_inc(ring_full, 1)

            def attend(k):
                pe.wait_ge(tT_out, k + 1)
                if k < PAIRS - 1:
                    pe.wait_ge(sim2_ready, 2 * k + 2)
                else:
                    pe.wait_ge(inv_kept, 1)
                for m in range(2):
                    if k == PAIRS - 1:
                        pe.wait_ge(sim2_last, 3 + m)
                    for b in range(2):
                        mm = pe.matmul(att_ps[64 * b:64 * b + 64, N:2 * N], tT[:, m, 64 * b:64 * b + 64],
                                       sim2[:, b, m, :], start=(m == 0), stop=(m == 1))
                mm.then_inc(att_done, 1)

            def turn_reach():
                pe.wait_ge(reach_ready, 1)
                pe.wait_ge(xT_out, PAIRS)
                pe.transpose(prep_ps[0:1, 0:128], reach[:, PAIRS:PAIRS + 1], ident).then_inc(reach_turned, 1)

            pe.wait_ge(warm_zeroed, 1)
            warm_up(14, out_ps[:, 0:N])
            pe.wait_ge(table_in, 16)
            group_means(GN1_FIRST)
            turn_weights()
            warm_up(6, out_ps[:, 0:N])
            convolve(0)
            group_means(GN1_REST)
            turn_offsets(0)
            turn_more_weights()
            warm_up(6, out_ps[:, 0:N])
            turn_image(0)
            warm_up(4, out_ps[:, 0:N])
            turn(0, 0)
            for k in range(PAIRS + 1):
                main, after = k < PAIRS, k >= 1
                ahead = k + 1 < PAIRS
                if ahead:
                    convolve(k + 1)
                if main:
                    turn(k, 1)
                if after and ahead:
                    group_means(gn2(k - 1))
                if main:
                    sample(k, 0)
                if k == PAIRS:
                    warm_up(3, samp_ps[:, 0, 0:N])
                if after and not ahead:
                    group_means(gn2(k - 1))
                if k == PAIRS:
                    warm_up(17, samp_ps[:, 0, 0:N])
                if main:
                    turn(k, 2)
                if ahead:
                    turn_offsets(k + 1)
                if main:
                    sample(k, 1)
                    turn(k, 3)
                if k == PAIRS:
                    norms_and_t_last()
                elif after:
                    norms_and_t(k - 1)
                if main:
                    sample(k, 2)
                if ahead:
                    turn_image(k + 1)
                if k == PAIRS - 1 and not general:
                    turn_reach()
                if k == PAIRS:
                    similarities_last()
                    spread_inverse()
                    warm_up(4, samp_ps[:, 0, 0:N])
                elif after:
                    similarities(k - 1)
                if main:
                    sample(k, 3)
                if after and k < PAIRS:
                    turn_t(k - 1)
                if ahead:
                    turn(k + 1, 0)
                if k == PAIRS - 1:
                    project(k)
                if after:
                    attend(k - 1)
                if k < PAIRS - 1:
                    project(k)

        @block.scalar
        def _(act):
            act.dma_start(table[:, 0:early], consts[:, 0:early]).then_inc(table_in, 16)
            act.dma_start(table[:, early:], consts[:, early:]).then_inc(table_rest_in, 16)
            act.wait_ge(zeroed, 2)
            nc.scalar.activation(warm[:], warm[:], ACT.Sigmoid)
            act.dma_start(wconv_nat[:, :, 0, :], w_conv[:, 0:LOW * C].rearrange("o (t c) -> o t c", c=C)).then_inc(wrest_in, 16)
            act.wait_ge(w_turned, 1)
            act.wait_ge(zeroed, 3)
            turned = att_ps[64:128, 0:TAPS * OFFC].rearrange("p (t o) -> p t o", o=OFFC)[:, :, 0:27]
            nc.scalar.copy(woff_T[64:128, :, OFFC:OFFC + 27], turned).then_inc(woff_ready, 1)

            def normalised_rows(k):
                act.wait_ge(gn_shift[0], 1 if k == 0 else 2)
                if k == 0:
                    act.wait_ge(zeroed, 5)
                if k >= 2:
                    act.wait_ge(xT_done, k - 1)
                nc.scalar.activation(grows[:, k % 2, 2:2 + H, :].rearrange("p r c -> p (r c)"), x_sb[:, k, :], ACT.Identity,
                                     bias=shift[:, 0, k:k + 1], scale=rstd[:, 0, k:k + 1]).then_inc(rows_ready, 1)

            def conv_bias(k):
                act.wait_ge(conv_done, k + 1)
                if k == 0:
                    act.wait_ge(bias_in, 64)
                if k >= 1:
                    act.wait_ge(off_turned, k)
                nc.scalar.activation(conv_sb[:], prep_ps[:, 0:HALF], ACT.Identity, bias=boff_col[:, 0:1]).then_inc(conv_out, 1)

            def weights_out():
                act.wait_ge(w_turned, 2)
                act.wait_ge(zeroed, 6)
                turned = ring[RING - 1]
                nc.scalar.copy(wconv_T[:].rearrange("p t o -> p (t o)"), turned[:, 0:C * LOW])
                nc.scalar.copy(w1_T[0:64, 0:64], turned[0:64, C * LOW:C * LOW + C])
                nc.scalar.copy(w1_T[64:128, 64:128], turned[64:128, C * LOW:C * LOW + C]).then_inc(wrest_ready, 1)

            def make_mask(k):
                act.wait_ge(off_turned, k + 1)
                offs = prep_ps[:, 128:256].rearrange("p (t o) -> p t o", o=OFFC)
                nc.scalar.activation(mask[:, k % 2], offs[:, :, 2 * TAPS:3 * TAPS], ACT.Sigmoid).then_inc(mask_ready, 1)

            def image_out(k):
                act.wait_ge(xT_done, k + 1)
                if k >= 2:
                    act.wait_ge(samp_done, TILES * (k - 1))
                n = len(BLOCK_ROWS) * 128
                nc.scalar.copy(xT[:, k % 2].rearrange("p w c -> p (w c)"), prep_ps[:, 0:n]).then_inc(xT_out, 1)

            def groups_out(k, tile):
                for g in range(GROUPS):
                    if tile_of_group(g) != tile or g in DVE_GROUPS:
                        continue
                    i = index["turn", k, g]
                    act.wait_ge(ring_full, i + 1)
                    if k >= 2:
                        act.wait_ge(samp_done, TILES * (k - 1))
                    dst = ST[:, k % 2].rearrange("p s w q -> p (s w q)")[:, 512 * g:512 * g + 512]
                    nc.scalar.copy(dst, ring[i % RING][:]).then_inc(ring_act, 1)

            def sampled_out(k, tile):
                j, b = divmod(tile, 2)
                act.wait_ge(samp_done, TILES * k + tile + 1)
                if k >= 2:
                    act.wait_ge(out_done, k - 1)
                dst = sampled[:, k % 2, b, :, HALF * j:HALF * j + HALF].rearrange("p t (a q) -> p a t q", a=2)
                src = samp_ps[:, :, 0:LOW * 64].rearrange("p a (t q) -> p a t q", t=LOW)
                nc.scalar.copy(dst, src).then_inc(samp_out, 1)

            def squares(k):
                act.wait_ge(g_ready[1], k + 1)
                if k >= 1:
                    act.wait_ge(norm_t_done, k)
                nc.scalar.activation(g2_sq[:], g2[:, k % 2, :], ACT.Square).then_inc(sq_ready, 1)

            def t_out(k):
                act.wait_ge(tT_done, k + 1)
                if k >= 1:
                    act.wait_ge(att_done, k)
                nc.scalar.copy(tT[:].rearrange("p m c -> p (m c)"), att_ps[:, 0:N]).then_inc(tT_out, 1)

            def relu_similarities(k):
                for b in range(2):
                    i = index["sim", k, b]
                    act.wait_ge(ring_full, i + 1)
                    if k >= 1:
                        act.wait_ge(sim2_ready, 2 * k)
                    nc.scalar.activation(sim[:, b].rearrange("p m n -> p (m n)"), ring[i % RING][:], ACT.Relu).then_inc(ring_act, 1)

            def relu_similarities_last():
                act.wait_ge(sim2_ready, 2 * (PAIRS - 1))
                for n in range(4):
                    i = index["sim", PAIRS - 1, n]
                    act.wait_ge(ring_full, i + 1)
                    nc.scalar.activation(sim[:, n // 2, n % 2], ring[i % RING][:, 0:N], ACT.Relu).then_inc(ring_act, 1)

            def inverse_out():
                act.wait_ge(inv_spread, 1)
                act.wait_ge(y_own, PAIRS - 1)
                nc.scalar.copy(inv_norm2[:], att_ps[:, 0:N]).then_inc(inv_kept, 1)

            normalised_rows(0)
            conv_bias(0)
            make_mask(0)
            weights_out()
            image_out(0)
            groups_out(0, 0)
            normalised_rows(1)
            for k in range(PAIRS + 1):
                main, after = k < PAIRS, k >= 1
                ahead = k + 1 < PAIRS
                if ahead:
                    conv_bias(k + 1)
                if main:
                    groups_out(k, 1)
                    sampled_out(k, 0)
                    groups_out(k, 2)
                if ahead:
                    make_mask(k + 1)
                if after:
                    squares(k - 1)
                if main:
                    sampled_out(k, 1)
                    groups_out(k, 3)
                    sampled_out(k, 2)
                if ahead:
                    image_out(k + 1)
                if k == PAIRS:
                    relu_similarities_last()
                    inverse_out()
                elif after:
                    relu_similarities(k - 1)
                if k + 2 < PAIRS:
                    normalised_rows(k + 2)
                if main:
                    sampled_out(k, 3)
                if after and k < PAIRS:
                    t_out(k - 1)
                if ahead:
                    groups_out(k + 1, 0)

        @block.vector
        def _(dve):
            nc.vector.memset(warm_w[:], 0.0).then_inc(warm_zeroed, 1)
            nc.vector.memset(samp_ps[64:128, 0, 0:64], 0.0).then_inc(samp_zeroed, 1)
            nc.vector.memset(samp_ps[0:64, 1, 64 * (LOW - 1):64 * LOW], 0.0).then_inc(samp_zeroed, 1)
            own = [0, 0]

            def statistics(i, k):
                if i == 0:
                    dve.wait_ge(x_in[k], 16)
                else:
                    dve.wait_ge(x1_ready, k + 1)
                src = (x_sb if i == 0 else x1_sb)[:, k, :]
                nc.vector.bn_stats(stats6[:, i, k, :], src).then_inc(gn_own[i], 1)
                own[i] += 1
                dve.wait_ge(gn_own[i], own[i])
                nc.vector.bn_aggr(mv[:, i, k, :], stats6[:, i, k, :]).then_inc(gn_mv[i], 1)

            def group_variance(part):
                i, n, lo, hi = part
                dve.wait_ge(gn_group[i], n + 1)
                nc.vector.tensor_copy(gmv[:, i, lo:hi, :], group_ps(part)).then_inc(gn_own[i], 1)
                nc.vector.tensor_tensor(gdiff[:, i, lo:hi], group_ps(part)[:, :, 0], mv[:, i, lo:hi, 0],
                                        ALU.subtract).then_inc(gn_own[i], 1)
                dve.wait_ge(gn_own[i], own[i] + 2)
                nc.vector.tensor_tensor(var[:, i, lo:hi], gdiff[:, i, lo:hi], gdiff[:, i, lo:hi], ALU.mult).then_inc(gn_own[i], 1)
                own[i] += 3
                dve.wait_ge(gn_own[i], own[i])
                nc.vector.scalar_tensor_tensor(out=var[:, i, lo:hi], in0=gmv[:, i, lo:hi, 1], scalar=EPS_GN,
                                               in1=var[:, i, lo:hi], op0=ALU.add, op1=ALU.add).then_inc(gn_var[i], 1)

            def scale_and_shift(part):
                i, n, lo, hi = part
                dve.wait_ge(gn_rstd[i], n + 1)
                nc.vector.scalar_tensor_tensor(out=shift[:, i, lo:hi], in0=gmv[:, i, lo:hi, 0], scalar=-1.0,
                                               in1=rstd[:, i, lo:hi], op0=ALU.mult, op1=ALU.mult).then_inc(gn_shift[i], 1)
                dve.wait_ge(gn_shift[i], n + 1)

            def normalise(i, k):
                if i == 0:
                    src, dst = x_sb[:, k, :].rearrange("p (h w) -> p h w", w=W), image(k)
                    if k == 0:
                        dve.wait_ge(zeroed, 4)
                    if k >= 2:
                        dve.wait_ge(xT_done, k - 1)
                else:
                    src, dst = x1_sb[:, k, :], g2[:, k % 2, :]
                nc.vector.tensor_scalar(dst, src, rstd[:, i, k:k + 1], shift[:, i, k:k + 1], ALU.mult, ALU.add).then_inc(g_ready[i], 1)

            def distances(k, j):
                if j == 0:
                    dve.wait_ge(mask_ready, k + 1)
                if k == 0 and j == 0:
                    dve.wait_ge(table_rest_in, 16)
                if k >= 2:
                    dve.wait_ge(S_pool, S_count(k - 2, TILES - 1, True))
                    dve.wait_ge(S_dve, S_count(k - 2, TILES - 1, False))
                offs = prep_ps[:, 128:256].rearrange("p (t o) -> p t o", o=OFFC)
                ty, tx = (h.rearrange("p (t s) r -> p t s r", s=TAPS) for h in hats_of(k, j))
                rows = cy[:, j, :] if general else cy_window
                for n, (t, of, size) in enumerate(((ty, rows, ROWS), (tx, cx, W))):
                    nc.vector.tensor_tensor(t, offs[:, 2 * j:2 * j + 2, TAPS * n:TAPS * n + TAPS].unsqueeze(3).to_broadcast([128, 2, TAPS, size]),
                                            of.unsqueeze(1).unsqueeze(1).to_broadcast([128, 2, TAPS, size]),
                                            ALU.add).then_inc(dist_ready, 1)
                if j == 1 and not general:
                    nc.vector.tensor_reduce(reach[:, k:k + 1], offs[:, :, 0:TAPS], AX.XY, ALU.max,
                                            apply_absolute_value=True).then_inc(reach_own, 1)

            def make_hats(k, js):
                dve.wait_ge(dist_ready, 4 * k + 2 * js[-1] + 2)
                h = hats[:, k % 2, js[0]:js[-1] + 1, :]
                bits = h.bitcast(mybir.dt.int32)
                nc.vector.tensor_scalar(bits, bits, 0x7FFFFFFF, None, ALU.bitwise_and).then_inc(abs_ready, 1)
                dve.wait_ge(abs_ready, hats_count(k, js[-1]))
                nc.vector.tensor_scalar(h, h, 1.0, -1.0, ALU.min, ALU.add).then_inc(hats_ready, 1)

            def farthest():
                dve.wait_ge(reach_own, PAIRS)
                nc.vector.tensor_reduce(reach[:, PAIRS:PAIRS + 1], reach[:, 0:PAIRS], AX.X, ALU.max).then_inc(reach_ready, 1)

            def set_far():
                dve.wait_ge(reach_turned, 1)
                nc.vector.tensor_reduce(reach[0:1, PAIRS + 1:PAIRS + 2], prep_ps[0:1, 0:128], AX.X, ALU.max).then_inc(reach_own, 1)
                dve.wait_ge(reach_own, PAIRS + 1)
                nc.vector.tensor_scalar(far, reach[0:1, PAIRS + 1:PAIRS + 2], float(REACH), None, ALU.is_gt).then_inc(far_set, 1)

            def multiply(k, tile):
                dve.wait_ge(hy_masked, hats_count(k, tile // 2))
                if k >= S_BUFS:
                    dve.wait_ge(ring_full, index["turn", k - S_BUFS, last_group(tile)] + 1)
                o, a, b = S_part(k, tile)
                nc.vector.tensor_tensor(o, a, b, ALU.mult).then_inc(S_dve, 1)

            def groups_out(k, tile):
                for g in range(GROUPS):
                    if tile_of_group(g) != tile or g not in DVE_GROUPS:
                        continue
                    i = index["turn", k, g]
                    dve.wait_ge(ring_full, i + 1)
                    if k >= 2:
                        dve.wait_ge(samp_done, TILES * (k - 1))
                    dst = ST[:, k % 2].rearrange("p s w q -> p (s w q)")[:, 512 * g:512 * g + 512]
                    nc.vector.tensor_copy(dst, ring[i % RING][:]).then_inc(ring_dve, 1)

            def residual(k):
                dve.wait_ge(out_done, k + 1)
                nc.vector.tensor_tensor(x1_sb[:, k, :], out_ps[:, 0:N], x_sb[:, k, :], ALU.add).then_inc(x1_ready, 1)

            def square_last():
                dve.wait_ge(att_done, PAIRS - 1)
                for n in range(4):
                    b, m = divmod(n, 2)
                    wait_emptied(dve, index["sim", PAIRS - 1, n])
                    nc.vector.tensor_tensor(sim2[:, b, m], sim[:, b, m], sim[:, b, m], ALU.mult).then_inc(sim2_last, 1)

            def scale_t_last():
                dve.wait_ge(norm_t_done, PAIRS)
                dve.wait_ge(b1_rows_in, 16)
                dve.wait_ge(tT_done, PAIRS - 1)
                dve.wait_ge(att_done, PAIRS - 1)
                norms = att_ps[:, N:2 * N].rearrange("p (s c) -> p s c", c=C)[:, :, 0]
                nc.vector.tensor_scalar(norm2[:, 0:4], norms, EPS_NORM2, None, ALU.max).then_inc(norm2_ready, 1)
                nc.vector.tensor_tensor(t_scaled[:].rearrange("p (m c) -> p m c", m=2), att_ps[:, 0:N].rearrange("p (m c) -> p m c", m=2),
                                        b1_rows[:].rearrange("p b c -> p (b c)").unsqueeze(1).to_broadcast([128, 2, 128]),
                                        ALU.add).then_inc(t_ready, 1)
                dve.wait_ge(norm2_ready, PAIRS)
                nc.vector.reciprocal(inv_pixel[:], norm2[:, 0:4]).then_inc(inv_ready, 1)
                dve.wait_ge(inv_ready, PAIRS)
                dve.wait_ge(t_ready, PAIRS)
                nc.vector.tensor_tensor(tT[:].rearrange("p m (b c) -> p (m b) c", b=2), t_scaled[:].rearrange("p (s c) -> p s c", c=C),
                                        inv_pixel[:].unsqueeze(2).to_broadcast([128, 4, C]), ALU.mult).then_inc(tT_out, 1)

            def scale_t(k):
                dve.wait_ge(norm_t_done, k + 1)
                if k >= 1:
                    dve.wait_ge(y_own, k)
                nc.vector.tensor_scalar(norm2[:], att_ps[:, 0:N], EPS_NORM2, None, ALU.max).then_inc(norm2_ready, 1)
                dve.wait_ge(norm2_ready, k + 1)
                nc.vector.reciprocal(inv_norm2[:], norm2[:]).then_inc(inv_ready, 1)
                dve.wait_ge(inv_ready, k + 1)
                if k == 0:
                    dve.wait_ge(b1_in, 32)
                if k >= 1:
                    dve.wait_ge(tT_done, k)
                nc.vector.scalar_tensor_tensor(out=t_scaled[:], in0=att_ps[:, N:2 * N], scalar=b1_col[:, 0:1],
                                               in1=inv_norm2[:], op0=ALU.add, op1=ALU.mult).then_inc(t_ready, 1)

            def scale_attended(k):
                dve.wait_ge(att_done, k + 1)
                if k == PAIRS - 1:
                    dve.wait_ge(inv_kept, 1)
                y = y_sb[:, k, :]
                nc.vector.tensor_tensor(y, att_ps[:, N:2 * N], inv_norm2[:], ALU.mult).then_inc(y_own, 1)

            def finish(k):
                y = y_sb[:, k, :]
                dve.wait_ge(y_own, k + 1)
                nc.vector.tensor_tensor(y, y, x1_sb[:, k, :], ALU.add).then_inc(y_ready, 1)

            statistics(0, 0)
            group_variance(GN1_FIRST)
            scale_and_shift(GN1_FIRST)
            normalise(0, 0)
            dve.wait_ge(w_turned, 1)
            dve.wait_ge(zeroed, 3)
            turned = att_ps[0:64, 0:TAPS * OFFC].rearrange("p (t o) -> p t o", o=OFFC)[:, :, 0:27]
            nc.vector.tensor_copy(woff_T[0:64, :, 0:27], turned).then_inc(woff_ready, 1)
            for k in range(1, PAIRS):
                statistics(0, k)
            group_variance(GN1_REST)
            distances(0, 0)
            make_hats(0, (0,))
            distances(0, 1)
            multiply(0, 0)
            make_hats(0, (1,))
            scale_and_shift(GN1_REST)
            normalise(0, 1)
            multiply(0, 2)
            groups_out(0, 0)
            for k in range(PAIRS + 1):
                main, after = k < PAIRS, k >= 1
                ahead = k + 1 < PAIRS
                if k == PAIRS - 1 and not general:
                    farthest()
                if after:
                    statistics(1, k - 1)
                if main:
                    groups_out(k, 1)
                    multiply(k, 3)
                if k == PAIRS:
                    scale_attended(k - 2)
                if after:
                    group_variance(gn2(k - 1))
                if k == PAIRS:
                    finish(k - 2)
                if after:
                    scale_and_shift(gn2(k - 1))
                    normalise(1, k - 1)
                if main:
                    groups_out(k, 2)
                if ahead:
                    distances(k + 1, 0)
                    distances(k + 1, 1)
                    make_hats(k + 1, (0, 1))
                if main:
                    groups_out(k, 3)
                if k == PAIRS:
                    scale_t_last()
                elif after:
                    scale_t(k - 1)
                if ahead:
                    multiply(k + 1, 0)
                if k + 2 < PAIRS:
                    normalise(0, k + 2)
                if k == PAIRS - 1 and not general:
                    set_far()
                if k == PAIRS:
                    square_last()
                if ahead:
                    multiply(k + 1, 2)
                    groups_out(k + 1, 0)
                if after and k != PAIRS - 1:
                    scale_attended(k - 1)
                    finish(k - 1)
                if main:
                    residual(k)
            if not general:
                dve.wait_ge(far_set, 1)


def build(nc, *args):
    with (nc.sbuf_tensor("far", [1, 1], mybir.dt.int32) as far, nc.sbuf_tensor("y_sb", [128, PAIRS, N], F32) as y_sb,
          nc.semaphore("stored") as stored):
        run_pairs(nc, False, far[:], y_sb, stored, *args)
        too_far = nc.values_load(far[:], min_val=0, max_val=1)
        with nc.If(too_far > 0):
            run_pairs(nc, True, None, y_sb, stored, *args)
        nc.sync.wait_ge(stored, 16 * PAIRS)


def kernel(x, L0_conv_w_off, L0_conv_b_off, L0_conv_w_conv, L1_conv_W, L1_conv_b):
    import concourse.bacc as bacc
    from concourse.bass_utils import run_bass_kernel_spmd

    nc = bacc.Bacc("TRN2", target_bir_lowering=False, num_devices=1)
    given = {"x": x, "w_off": L0_conv_w_off, "b_off": L0_conv_b_off, "w_conv": L0_conv_w_conv,
             "w1": L1_conv_W, "b1": L1_conv_b, "consts": constants()}
    arrays = {name: np.ascontiguousarray(a) for name, a in given.items()}
    args = [nc.dram_tensor(name, a.shape, mybir.dt.from_np(a.dtype), kind="ExternalInput").ap()
            for name, a in arrays.items()]
    out = nc.dram_tensor("out", (B, C, H, W), F32, kind="ExternalOutput").ap()
    build(nc, *args, out)
    result = run_bass_kernel_spmd(nc, [arrays], core_ids=[0])
    return result.results[0]["out"]
```
